# Optimizing a Trainium2 kernel written in Bass

```python
import numpy as np
import jax
import jax.numpy as jnp

def _softmax(x, axis=-1):
    return jax.nn.softmax(x, axis=axis)

def _gelu(x):
    return jax.nn.gelu(x, approximate=True)

def _silu(x):
    return jax.nn.silu(x)

def _sigmoid(x):
    return jax.nn.sigmoid(x)

def _layernorm(x, axis=-1, eps=1e-05):
    m = jnp.mean(x, axis=axis, keepdims=True)
    v = jnp.var(x, axis=axis, keepdims=True)
    return (x - m) / jnp.sqrt(v + eps)

def _scatter_add(tgt, idx, src, axis=0):
    return tgt.at[idx].add(src)

def _segment_sum(src, seg, n):
    return jax.ops.segment_sum(src, seg, n)
kernel_name = 'mk_gnn_ffn_d1_gnn_r64_4619fe'

def setup_inputs(seed: int=0):
    np.random.seed(seed)
    _w = jnp.asarray

    def _rec_inputs():
        import jax
        import jax.numpy as jnp
        _gk = jax.random.key(seed)
        x = -6.415e-05 + 1 * jax.random.normal(jax.random.fold_in(_gk, 1), (10000, 1024), jnp.float32)
        _s = jax.random.randint(jax.random.fold_in(_gk, 2), (1250,), 0, 10000, jnp.int32)
        _d = jax.random.randint(jax.random.fold_in(_gk, 3), (1250,), 0, 10000, jnp.int32)
        _loop = jnp.arange(10000, dtype=jnp.int32)
        src = jnp.concatenate([_s, _d, _loop])
        dst = jnp.concatenate([_d, _s, _loop])
        _o = jnp.argsort(dst, stable=True)
        src = src[_o]
        dst = dst[_o]
        return (x, src, dst)
    x, src, dst = _rec_inputs()

    def _L0_gnn_setup():
        import jax, jax.numpy as jnp
        import numpy as np
        N_NODES = 10000
        N_EDGES = 2500
        DIM = 1024
        key = jax.random.key(seed)
        k1, k2, k3 = jax.random.split(key, 3)
        x = jax.random.normal(k1, (N_NODES, DIM), dtype=jnp.float32)
        edge_index = jax.random.randint(k2, (2, N_EDGES), 0, N_NODES, dtype=jnp.int64)
        W = jax.random.normal(k3, (DIM, DIM), dtype=jnp.float32) * (1.0 / np.sqrt(DIM))
        b = jnp.zeros((DIM,), dtype=jnp.float32)
        return {'x': x, 'edge_index': edge_index, 'W': W, 'b': b}
    _L0_gnn_all = _L0_gnn_setup()
    _L0_gnn_in = {k: v for k, v in _L0_gnn_all.items() if k in ('W', 'b')}
    del _L0_gnn_all

    def _L0_ffn_setup():
        import jax, jax.numpy as jnp
        import numpy as np
        D_MODEL, D_FF, RANK = (1024, 64, 256)
        B, S = (4, 64)
        key = jax.random.key(seed)
        ks = jax.random.split(key, 7)
        return {'x': jax.random.normal(ks[0], (B, S, D_MODEL), dtype=jnp.float32), 'U1': jax.random.normal(ks[1], (D_MODEL, RANK), dtype=jnp.float32) * 0.02, 'V1': jax.random.normal(ks[2], (RANK, D_FF), dtype=jnp.float32) * 0.02, 'b1': jnp.zeros((D_FF,), dtype=jnp.float32), 'U2': jax.random.normal(ks[3], (D_FF, RANK), dtype=jnp.float32) * 0.02, 'V2': jax.random.normal(ks[4], (RANK, D_MODEL), dtype=jnp.float32) * 0.02, 'b2': jnp.zeros((D_MODEL,), dtype=jnp.float32)}
    _L0_ffn_all = _L0_ffn_setup()
    _L0_ffn_in = {k: v for k, v in _L0_ffn_all.items() if k in ('U1', 'V1', 'b1', 'U2', 'V2', 'b2')}
    del _L0_ffn_all
    return {'x': x, 'src': src, 'dst': dst, 'L0_gnn_W': _L0_gnn_in['W'], 'L0_gnn_b': _L0_gnn_in['b'], 'L0_ffn_U1': _L0_ffn_in['U1'], 'L0_ffn_V1': _L0_ffn_in['V1'], 'L0_ffn_b1': _L0_ffn_in['b1'], 'L0_ffn_U2': _L0_ffn_in['U2'], 'L0_ffn_V2': _L0_ffn_in['V2'], 'L0_ffn_b2': _L0_ffn_in['b2']}

def reference(x, src, dst, L0_gnn_W, L0_gnn_b, L0_ffn_U1, L0_ffn_V1, L0_ffn_b1, L0_ffn_U2, L0_ffn_V2, L0_ffn_b2):
    import jax
    import jax.numpy as jnp

    def _L0_gnn_ref(x, edge_index, W, b):
        import jax, jax.numpy as jnp
        import numpy as np
        N_NODES = 10000
        N_EDGES = 2500
        DIM = 1024
        'GCNConv (add_self_loops=True, symmetric norm) -> Dropout(eval=identity) -> ReLU.'
        n = x.shape[0]
        loops = jnp.arange(n, dtype=edge_index.dtype)
        src = jnp.concatenate([edge_index[0], loops])
        dst = jnp.concatenate([edge_index[1], loops])
        deg = jax.ops.segment_sum(jnp.ones_like(dst, dtype=x.dtype), dst, num_segments=n)
        dinv = jnp.where(deg > 0, jax.lax.rsqrt(deg), jnp.zeros_like(deg))
        norm = dinv[src] * dinv[dst]
        h = x @ W
        msg = h[src] * norm[:, None]
        out = jax.ops.segment_sum(msg, dst, num_segments=n) + b
        return jax.nn.relu(out)

    def _L0_ffn_ref(x, U1, V1, b1, U2, V2, b2):
        import jax, jax.numpy as jnp
        import numpy as np
        D_MODEL, D_FF, RANK = (1024, 64, 256)
        B, S = (4, 64)
        P = jnp.einsum('bsd,dr->bsr', x, U1)
        H = jax.nn.gelu(jnp.einsum('bsr,rf->bsf', P, V1) + b1)
        Q = jnp.einsum('bsf,fr->bsr', H, U2)
        return jnp.einsum('bsr,rd->bsd', Q, V2) + b2
    edge_index = jnp.stack([src, dst])
    x = x + _L0_gnn_ref(_layernorm(x, axis=-1), edge_index, L0_gnn_W, L0_gnn_b)
    x = x + _L0_ffn_ref(_layernorm(x, axis=-1)[None], L0_ffn_U1, L0_ffn_V1, L0_ffn_b1, L0_ffn_U2, L0_ffn_V2, L0_ffn_b2)[0]
    return x

_drawn_inputs = setup_inputs


def setup_inputs(seed=0):
    import zlib

    import numpy as np

    out = dict(_drawn_inputs(seed))
    spreads = {'L0_gnn_b': (0.0, 0.1), 'L0_ffn_b1': (0.0, 0.8), 'L0_ffn_b2': (0.0, 2.0)}
    factors = {'L0_ffn_U1': 8.0, 'L0_ffn_V1': 8.0, 'L0_ffn_U2': 8.0, 'L0_ffn_V2': 8.0}
    for name, (base, spread) in spreads.items():
        noise = np.random.default_rng([zlib.crc32(name.encode()), seed]).standard_normal(out[name].shape)
        drawn = base * np.exp(spread * noise) if base else spread * noise
        out[name] = jnp.asarray(drawn.astype(out[name].dtype))
    for name, factor in factors.items():
        out[name] = (out[name] * factor).astype(out[name].dtype)
    return out
```

```python
from contextlib import ExitStack

import concourse.bass as bass
from concourse import mybir



def gcn_ffn(nc, x, src, dst, W, b, U1, V1, b1, U2, V2, b2, out):
    F32, F32R, F16, I32 = mybir.dt.float32, mybir.dt.float32r, mybir.dt.float16, mybir.dt.int32
    ALU = mybir.AluOpType
    ACT = mybir.ActivationFunctionType
    AX = mybir.AxisListType

    P = 128
    N, D = x.shape
    E = src.shape[0]
    RANK, FF = V1.shape
    EPS = 1e-5
    NT = (N + P - 1) // P
    LAST = N - (NT - 1) * P
    EP = max(p for p in range(1, P + 1) if E % p == 0)
    EC = E // EP
    KC = D // P
    RC = RANK // P
    H2 = D // 2
    SLOTS = P // 2
    WB = 4
    B = 3
    BIG = 1000.0
    GROUP = 5
    assert EC % (2 * GROUP) == 0 and EC >= 4 * GROUP and GROUP * NT <= H2 and N <= 7 * 2048 and D == 1024 and FF <= 64 and H2 == 512

    ctx = ExitStack()
    with ctx:
        def sb(name, shape, dt):
            return ctx.enter_context(nc.sbuf_tensor(name, shape, dt))

        def sem(name):
            return ctx.enter_context(nc.semaphore(name))

        w_hi = sb("w_hi", [P, KC, D], F32R)
        w_lo = sb("w_lo", [P, KC, D], F32R)
        yt_hi = sb("yt_hi", [P, B, D], F32R)
        yt_lo = sb("yt_lo", [P, B, D], F32R)
        in_tile = sb("in_tile", [P, NT * EC], F16)
        gn_hi_t = in_tile[:, 0:2 * D].bitcast(F32R)
        in_tile3 = in_tile[:, :].rearrange("p (t c) -> p t c", c=EC)

        shared = sb("shared", [P, 18 * D], F32)
        x_t = shared[:, 0:3 * D].rearrange("p (b d) -> p b d", b=B)
        z_t = shared[:, 3 * D:4 * D]
        x1_t = shared[:, 4 * D:7 * D].rearrange("p (b d) -> p b d", b=B)
        gn_t = shared[:, 7 * D:8 * D]
        xs_t = shared[:, 8 * D:9 * D]
        y_t = shared[:, 9 * D:10 * D]
        x1n_t = shared[:, 10 * D:11 * D]
        xt_t = shared[:, 11 * D:12 * D]
        b_all = shared[:, 12 * D:13 * D]
        og_t = shared[:, 13 * D:14 * D]
        on_t = shared[:, 14 * D:15 * D]
        g_t = shared[:, 15 * D:18 * D].rearrange("p (b d) -> p b d", b=B)
        not_first = shared[:, 0:4 * D].bitcast(F16)[0:EP, 0:NT * EC]
        count = shared[:, 4 * D:8 * D].bitcast(F16)[0:EP, 0:NT * EC]
        count3 = count.rearrange("p (t c) -> p t c", c=EC)
        u1T = shared[:, 4 * D:6 * D].rearrange("p (r n) -> p r n", r=RC)
        v2_t = shared[:, 6 * D:8 * D].rearrange("p (r n) -> p r n", r=RC)
        w_stage = shared[:, 8 * D:12 * D].rearrange("p (k n) -> p k n", k=WB)
        hots = shared[:, 8 * D:12 * D].bitcast(F16)
        node_hot = hots[:, 0:2 * GROUP * P].rearrange("p (b g n) -> p b g n", b=2, g=GROUP)
        loop_hot = hots[:, 2 * D:2 * D + 2 * GROUP * NT].rearrange("p (b g n) -> p b g n", b=2, g=GROUP)
        slot_hot = hots[:, 4 * D:4 * D + 2 * GROUP * SLOTS].rearrange("p (b g n) -> p b g n", b=2, g=GROUP)
        slot_val = hots[:, 5 * D:5 * D + 4 * GROUP * SLOTS].rearrange("p (b g v n) -> p b g v n", b=2, g=GROUP, v=2)
        u1_t = shared[:, 12 * D:14 * D].rearrange("p (k r) -> p k r", k=KC)
        u2_t = shared[:, 14 * D:14 * D + RANK]
        v1_t = shared[:, 14 * D + 256:14 * D + 256 + RC * FF].rearrange("p (r f) -> p r f", r=RC)
        u2T = shared[:, 14 * D + 512:14 * D + 512 + RC * 2 * FF].rearrange("p (r c f) -> p r c f", r=RC, c=2)
        b2_t = shared[:, 15 * D:16 * D]
        edge = [shared[:, 16 * D + i * EC:16 * D + (i + 1) * EC] for i in range(11)]
        tile_i, low_i, shi_e, dst_i, top_i, digit_i = (a.bitcast(I32) for a in edge[0:6])
        tile_f, loop_f, tile_lp, digit1, digit2 = edge[6:11]
        assert NT * EC <= 8 * D and 11 * EC <= 2 * D and KC * RANK <= 2 * D and RC * D <= 2 * D
        assert RC * FF <= 256 and RANK <= 256 and 4 * GROUP * SLOTS <= 2 * D and 2 * GROUP * P <= 2 * D and FF == 64

        gn_r = sb("gn_r", [P, D], F32R)
        uv1 = sb("uv1", [P, KC, 2, FF], F32)
        uv2_a = sb("uv2_a", [P, D], F32R)
        uv2_b = sb("uv2_b", [P, D], F32R)
        b1_t = sb("b1_t", [P, 1], F32)
        h_t = sb("h_t", [P, P], F32)
        h_a = sb("h_a", [P, P], F32R)
        h_b = sb("h_b", [P, P], F32R)
        tq = sb("tq", [P, NT], F32)
        ident = sb("ident", [P, P], F32)
        below = sb("below", [P, P], F16)
        iota_t = sb("iota_t", [P, NT], F32)
        iota_t16 = sb("iota_t16", [P, NT], F16)
        iota_self = sb("iota_self", [P, NT], F16)
        iota_1 = sb("iota_1", [P, P], F32)
        iota_16 = sb("iota_16", [P, P], F16)
        src_i = sb("src_i", [P, EC + 1], I32)
        didx_e = sb("didx_e", [P, EC + 1], I32)
        low1 = sb("low1", [P, EC], F32)
        tile_nb = sb("tile_nb", [P, EC], F32)
        rank1 = sb("rank1", [P, EC], F32)
        nb_src = sb("nb_src", [P, NT], I32)
        nb_from = sb("nb_from", [P, NT], I32)
        nb_lo = sb("nb_lo", [P, NT], I32)
        nb_hi = sb("nb_hi", [P, NT], I32)
        nb_didx = sb("nb_didx", [P, NT], I32)
        empty = sb("empty", [P, NT], F32)
        nb_row = sb("nb_row", [P, NT], F32)
        loops1 = sb("loops1", [P, NT], F32)
        deg = sb("deg", [P, NT], F32)
        dinv = sb("dinv", [P, NT], F32)
        dinv_a = sb("dinv_a", [P, NT], F32)
        dinv_y = sb("dinv_y", [P, NT], F32)
        dinv2 = sb("dinv2", [P, NT], F32)
        own = sb("own", [P, NT], F32)
        code_i = sb("code_i", [P, NT], I32)
        base_t = sb("base_t", [P, NT], F32)
        most = sb("most", [P, 1], F32)
        most_row = sb("most_row", [1, 1], F32)
        over_i = sb("over_i", [1, 1], I32)
        ag_st = sb("ag_st", [P, 2, 2, 6], F32)
        ag_mv = sb("ag_mv", [P, 2, 2], F32)
        ag_v = sb("ag_v", [P, 2], F32)
        ag_a = sb("ag_a", [P, 2], F32)
        ag_y = sb("ag_y", [P, 2], F32)
        x_sc = sb("x_sc", [P, B, 1], F32)
        x_bi = sb("x_bi", [P, B, 1], F32)
        g_sc = sb("g_sc", [P, B, 1], F32)
        g_bi = sb("g_bi", [P, B, 1], F32)
        f_st = sb("f_st", [P, 2, 6], F32)
        f_mv = sb("f_mv", [P, 2], F32)
        f_v = sb("f_v", [P, 1], F32)
        f_a = sb("f_a", [P, 1], F32)
        f_y = sb("f_y", [P, 1], F32)
        f_sc = sb("f_sc", [P, B, 1], F32)
        f_bi = sb("f_bi", [P, B, 1], F32)
        idx_src = sb("idx_src", [P, B], I32)
        idx_dinv = sb("idx_dinv", [P, B], I32)
        g_dinv = sb("g_dinv", [P, B], F32)
        spread = sb("spread", [P, B, P], F32R)
        o_src = sb("o_src", [P, 2], I32)
        o_didx = sb("o_didx", [P, 2], I32)
        o_dinv = sb("o_dinv", [P, 1], F32)
        o_st = sb("o_st", [P, 2, 6], F32)
        o_mv = sb("o_mv", [P, 2], F32)
        o_v = sb("o_v", [P, 1], F32)
        o_a = sb("o_a", [P, 1], F32)
        o_y = sb("o_y", [P, 1], F32)
        o_sc = sb("o_sc", [P, 1], F32)
        o_late = sb("o_late", [P, 1], F32)
        o_mine = sb("o_mine", [P, 1], F32)
        o_hot = sb("o_hot", [P, P], F32)

        ps_a = ctx.enter_context(nc.psum_tensor("ps_a", [P, D], F32))
        ps_z = ctx.enter_context(nc.psum_tensor("ps_z", [P, D], F32))
        ps_t = ctx.enter_context(nc.psum_tensor("ps_t", [P, D], F32))
        ps_q = ctx.enter_context(nc.psum_tensor("ps_q", [P, D], F32))
        dinv_dram = nc.dram_tensor("dinv_dram", [P * NT, 1], F32, kind="Internal").ap()

        src_in, dst_in, u_in, b_in = sem("src_in"), sem("dst_in"), sem("u_in"), sem("b_in")
        w_in = [sem(f"w_in{k}") for k in range(KC)]
        consts = sem("consts")
        prep = sem("prep")
        tiles_ready = sem("tiles_ready")
        mask_ready = sem("mask_ready")
        ident_ready = sem("ident_ready")
        u1T_ps, u1T_sb, u2T_ps, u2T_sb = sem("u1T_ps"), sem("u1T_sb"), sem("u2T_ps"), sem("u2T_sb")
        uv1_ps, uv2_ps, uv_ready = sem("uv1_ps"), sem("uv2_ps"), sem("uv_ready")
        w_hi_ready, w_lo_ready = sem("w_hi_ready"), sem("w_lo_ready")
        count_in, base_ready = sem("count_in"), sem("base_ready")
        scanned, digits_ready = sem("scanned"), sem("digits_ready")
        b2_in, uv2_part, slot_val_ready = sem("b2_in"), sem("uv2_part"), sem("slot_val_ready")
        tq_ready, digits_ps = sem("tq_ready"), sem("digits_ps")
        hot_ready, hot_used = sem("hot_ready"), sem("hot_used")
        slot_ready, slot_used = sem("slot_ready"), sem("slot_used")
        most_ready, most_ps = sem("most_ready"), sem("most_ps")
        over_ready = sem("over_ready")
        tables_ready = sem("tables_ready")
        dinv_out = sem("dinv_out")
        g_zero = sem("g_zero")
        h_one = sem("h_one")
        gn_hi, gn_lo, h_gelu, h_hi = sem("gn_hi"), sem("gn_lo"), sem("h_gelu"), sem("h_hi")
        x_in = [sem(f"x_in{j}") for j in range(B)]
        g_in = [sem(f"g_in{j}") for j in range(B)]
        d_in = [sem(f"d_in{j}") for j in range(B)]
        out_done = [sem(f"out_done{j}") for j in range(B)]
        idx_ready = sem("idx_ready")
        coef_link, f_link = sem("coef_link"), sem("f_link")
        x_coef, g_coef, f_coef, f_stats = sem("x_coef"), sem("g_coef"), sem("f_coef"), sem("f_stats")
        spread_ready, gn_ready, xs_ready = sem("spread_ready"), sem("gn_ready"), sem("xs_ready")
        nb_sum, y_ready, yT_ps, yT_hi, yT_lo = (sem(n) for n in ("nb_sum", "y_ready", "yT_ps", "yT_hi", "yT_lo"))
        z_ps, z_biased, z_relu, x1_ready, x1n_ready = (sem(n) for n in ("z_ps", "z_biased", "z_relu", "x1_ready", "x1n_ready"))
        xT_ps, xT_ready, h_ps, h_ready, q_ps, out_ready = (sem(n) for n in ("xT_ps", "xT_ready", "h_ps", "h_ready", "q_ps", "out_ready"))
        o_idx, o_in, o_din, o_chain, o_ready, o_used = (sem(n) for n in ("o_idx", "o_in", "o_din", "o_chain", "o_ready", "o_used"))

        block = ctx.enter_context(nc.Block())

        def tile(m, j, shift):
            j += shift
            return m + j // B, j % B

        def number(m, j):
            return m * B + j

        def steps(eng, step):
            first, last = 2, (NT - 5) // B
            for i in range(-2, B * first):
                step(i // B, i % B)
            with eng.Fori(first, last) as m:
                for j in range(B):
                    step(m, j)
            for i in range(B * last, NT + 2):
                step(i // B, i % B)

        def exists(m, j):
            return not isinstance(m, int) or 0 <= number(m, j) < NT

        def wait(eng, s, value):
            if not isinstance(value, int) or value > 0:
                eng.wait_ge(s, value)

        @block.sync
        def _(sp):
            sp.dma_start(dst_i[0:EP, :], dst.rearrange("(p c) -> p c", p=EP)).then_inc(dst_in, 16)
            sp.dma_start(src_i[0:EP, 0:EC], src.rearrange("(p c) -> p c", p=EP)).then_inc(src_in, 16)
            sp.dma_start(u1_t, U1.rearrange("(k p) r -> p k r", p=P)).then_inc(u_in, 16)
            sp.dma_start(u2_t[0:FF, :], U2).then_inc(u_in, 16)
            sp.dma_start(v1_t, V1.rearrange("(r p) f -> p r f", p=P)).then_inc(u_in, 16)
            sp.dma_start(v2_t, V2.rearrange("(r p) n -> p r n", p=P)).then_inc(u_in, 16)
            for half in range(2):
                sp.dma_start(b1_t[half * FF:(half + 1) * FF, :], b1.rearrange("(f o) -> f o", o=1)).then_inc(b_in, 16)
            for row in (64, 96):
                sp.dma_start(b2_t[row:row + 1, :], b2.rearrange("(o n) -> o n", o=1)).then_inc(b2_in, 16)
            for k in range(KC):
                if k >= WB:
                    sp.wait_ge(w_lo_ready, k - WB + 1)
                sp.dma_start(w_stage[:, k % WB, :], W[k * P:(k + 1) * P, :]).then_inc(w_in[k], 16)
            sp.wait_ge(tables_ready, 1)
            sp.dma_start(dinv_dram.rearrange("(p t) o -> p (t o)", p=P), dinv[:, :]).then_inc(dinv_out, 16)
            sp.dma_start(b_all, b.rearrange("(o n) -> o n", o=1).broadcast_to([P, D])).then_inc(b_in, 16)

            def load(m, j):
                rows = LAST if isinstance(m, int) and number(m, j) == NT - 1 else P
                wait(sp, x1_ready, number(m, j) - B + 1)
                sp.dma_start(x_t[0:rows, j, :], x[bass.ds(number(m, j) * P, rows), :]).then_inc(x_in[j], 16)

            def store(m, j):
                rows = LAST if isinstance(m, int) and number(m, j) == NT - 1 else P
                sp.wait_ge(out_ready, number(m, j) + 1)
                sp.dma_start(out[bass.ds(number(m, j) * P, rows), :], x1_t[0:rows, j, :]).then_inc(out_done[j], 16)

            load(0, 0)

            def step(m, j):
                for shift, what in ((-2, store), (3, load)):
                    tm, tj = tile(m, j, shift)
                    if exists(tm, tj):
                        what(tm, tj)

            steps(sp, step)
            for j in range(B):
                sp.wait_ge(out_done[j], 16 * len(range(j, NT, B)))
            sp.wait_ge(dinv_out, 16)

        @block.gpsimd
        def _(pool):
            pool.memset(ident[:, :], 0.0).then_inc(ident_ready, 1)
            pool.memset(below[:, :], 0.0).then_inc(ident_ready, 1)
            pool.wait_ge(ident_ready, 2)
            pool.affine_select(out=ident[:, :], in_=ident[:, :], compare_op=ALU.not_equal, fill=1.0, base=0,
                               pattern=[[-1, P]], channel_multiplier=1).then_inc(ident_ready, 1)
            pool.affine_select(out=below[:, :], in_=below[:, :], compare_op=ALU.is_ge, fill=1.0, base=0,
                               pattern=[[-1, P]], channel_multiplier=1).then_inc(ident_ready, 1)
            for table, base in ((iota_t, 0), (iota_t16, 0), (iota_self, int(BIG)), (iota_1, 1), (iota_16, 1)):
                pool.iota(table[:, :], [[1, table.shape[1]]], base=base, channel_multiplier=0,
                          allow_small_or_imprecise_dtypes=True).then_inc(consts, 1)
            pool.memset(not_first, 1.0).then_inc(mask_ready, 1)
            pool.wait_ge(mask_ready, 1)
            pool.memset(not_first.rearrange("p (t c) -> p t c", c=EC)[:, :, 0:1], 0.0).then_inc(mask_ready, 1)
            pool.memset(h_b[:, :].bitcast(F32), 1.0).then_inc(h_one, 1)
            pool.memset(uv2_b[:, :].bitcast(F32), 0.0).then_inc(h_one, 1)
            for k in range(KC):
                pool.wait_ge(w_hi_ready, k + 1)
                pool.tensor_tensor(w_lo[:, k, :], w_stage[:, k % WB, :], w_hi[:, k, :].bitcast(F32),
                                   ALU.subtract).then_inc(w_lo_ready, 1)

            def slot_values(q):
                for r in range(2):
                    g = q * 2 + r
                    wait(pool, slot_used, g - 1)
                    pool.wait_ge(slot_ready, g + 1)
                    for v, digit in enumerate((digit1, digit2)):
                        pool.tensor_tensor(slot_val[0:EP, r, :, v, :], slot_hot[0:EP, r],
                                           digit[0:EP, bass.ds(g * GROUP, GROUP), None].to_broadcast([EP, GROUP, SLOTS]),
                                           ALU.mult).then_inc(slot_val_ready, 1)

            slot_values(0)
            with pool.Fori(1, EC // (2 * GROUP)) as q:
                slot_values(q)
            pool.wait_ge(tables_ready, 1)
            pool.memset(shared[:, 15 * D:18 * D], 0.0).then_inc(g_zero, 1)
            pool.memset(in_tile[:, 0:2 * D].bitcast(F32), 0.0).then_inc(g_zero, 1)
            pool.memset(g_dinv[:, :], 0.0).then_inc(g_zero, 1)
            pool.wait_ge(g_zero, 3)
            pool.wait_ge(dinv_out, 16)

            last_row = pool.to_reg(N - 1)
            last_dinv = pool.to_reg(P * NT - 1)

            def stage(m, j):
                t = number(m, j)
                wait(pool, g_in[j], m * 16)
                wait(pool, d_in[j], m * 16)
                pool.tensor_copy(idx_src[:, j:j + 1], nb_src[:, bass.ds(t, 1)]).then_inc(idx_ready, 1)
                pool.tensor_copy(idx_dinv[:, j:j + 1], nb_didx[:, bass.ds(t, 1)]).then_inc(idx_ready, 1)

            def gather(m, j):
                t = number(m, j)
                pool.wait_ge(idx_ready, t * 2 + 2)
                wait(pool, gn_ready, t - B + 1)
                if exists(*tile(m, j, 1)):
                    stage(*tile(m, j, 1))
                pool.indirect_dma_start(
                    out=g_t[:, j, :], out_offset=None, in_=x,
                    in_offset=bass.IndirectOffsetOnAxis(ap=idx_src[:, j:j + 1], axis=0),
                    bounds_check=last_row, oob_is_err=False).then_inc(g_in[j], 16)
                pool.indirect_dma_start(
                    out=g_dinv[:, j:j + 1], out_offset=None, in_=dinv_dram,
                    in_offset=bass.IndirectOffsetOnAxis(ap=idx_dinv[:, j:j + 1], axis=0),
                    bounds_check=last_dinv, oob_is_err=False).then_inc(d_in[j], 16)

            def low_rows(m, j):
                t = number(m, j)
                pool.wait_ge(gn_ready, t + 1)
                pool.wait_ge(gn_hi, t + 1)
                wait(pool, nb_sum, t)
                pool.tensor_tensor(gn_r[:, :], gn_t, gn_hi_t.bitcast(F32),
                                   ALU.subtract).then_inc(gn_lo, 1)

            def residual(m, j):
                t = number(m, j)
                pool.wait_ge(z_relu, t + 1)
                wait(pool, out_done[j], m * 16)
                pool.tensor_tensor(x1_t[:, j, :], z_t, x_t[:, j, :], ALU.add).then_inc(x1_ready, 1)

            def general(m, j):
                t = number(m, j)
                with pool.Fori(0, EC // 2) as q:
                    for r in range(2):
                        n = t * EC + q * 2 + r
                        pool.wait_ge(o_idx, n * 2 + 2)
                        pool.wait_ge(o_ready, n + 1)
                        stage_edges(q * 2 + r + 1, 1 - r)
                        pool.indirect_dma_start(
                            out=og_t[0:EP, :], out_offset=None, in_=x,
                            in_offset=bass.IndirectOffsetOnAxis(ap=o_src[0:EP, r:r + 1], axis=0),
                            bounds_check=last_row, oob_is_err=False).then_inc(o_in, 16)
                        pool.indirect_dma_start(
                            out=o_dinv[0:EP, :], out_offset=None, in_=dinv_dram,
                            in_offset=bass.IndirectOffsetOnAxis(ap=o_didx[0:EP, r:r + 1], axis=0),
                            bounds_check=last_dinv, oob_is_err=False).then_inc(o_din, 16)

            def stage_edges(c, r):
                pool.tensor_copy(o_src[0:EP, r:r + 1], src_i[0:EP, bass.ds(c, 1)]).then_inc(o_idx, 1)
                pool.tensor_copy(o_didx[0:EP, r:r + 1], didx_e[0:EP, bass.ds(c, 1)]).then_inc(o_idx, 1)

            def main(over):
                stage(0, 0)
                if over:
                    stage_edges(0, 0)
                for t in range(2):
                    gather(0, t)

                def step(m, j):
                    tm, tj = tile(m, j, -1)
                    if exists(tm, tj):
                        residual(tm, tj)
                    tm, tj = tile(m, j, 1)
                    if over and exists(tm, tj):
                        general(tm, tj)
                    tm, tj = tile(m, j, 4)
                    if exists(tm, tj):
                        gather(tm, tj)
                    tm, tj = tile(m, j, 2)
                    if exists(tm, tj):
                        low_rows(tm, tj)

                steps(pool, step)

            pool.wait_ge(over_ready, 1)
            over = pool.value_load(over_i[0:1, 0:1], min_val=0, max_val=1)
            with pool.If(over > 0):
                main(True)
            with pool.Else():
                main(False)

        @block.scalar
        def _(act):
            act.wait_ge(u1T_ps, 1)
            act.copy(u1T[:, 0, :], ps_t[:, :]).then_inc(u1T_sb, 1)
            act.copy(u1T[:, 1, :], ps_q[:, :]).then_inc(u1T_sb, 1)
            act.wait_ge(u2T_ps, 1)
            for c in range(2):
                act.copy(u2T[:, :, c, :], ps_z[:, 0:RC * FF].rearrange("p (r f) -> p r f", r=RC)).then_inc(u2T_sb, 1)
            for k in range(KC):
                act.wait_ge(w_in[k], 16)
                act.copy(w_hi[:, k, :], w_stage[:, k % WB, :]).then_inc(w_hi_ready, 1)
            act.wait_ge(uv1_ps, 1)
            for c in range(2):
                act.copy(uv1[:, :, c, :], ps_t[:, 0:KC * FF].rearrange("p (k f) -> p k f", k=KC)).then_inc(uv_ready, 1)
            act.wait_ge(uv2_ps, 1)
            act.copy(uv2_a[:, :], ps_q[:, :]).then_inc(uv_ready, 1)
            act.wait_ge(b2_in, 32)
            act.wait_ge(h_one, 2)
            for row in (64, 96):
                act.copy(uv2_b[row:row + 1, :], b2_t[row:row + 1, :]).then_inc(uv_ready, 1)

            def high_rows(m, j):
                t = number(m, j)
                act.wait_ge(gn_ready, t + 1)
                wait(act, gn_lo, t)
                act.copy(gn_hi_t[SLOTS:P, :], gn_t[SLOTS:P, :]).then_inc(gn_hi, 1)

            def own_rows(m, j):
                t = number(m, j)
                act.wait_ge(x_coef, t + 1)
                wait(act, y_ready, t)
                act.activation(xs_t, x_t[:, j, :], ACT.Identity, bias=x_bi[:, j, :],
                               scale=x_sc[:, j, :]).then_inc(xs_ready, 1)

            def high_part(m, j):
                t = number(m, j)
                act.wait_ge(yT_ps, t + 1)
                wait(act, z_ps, t - B + 1)
                act.copy(yt_hi[:, j, :], ps_t[:, :]).then_inc(yT_hi, 1)

            def relu(m, j):
                t = number(m, j)
                act.wait_ge(z_biased, t + 1)
                act.activation(z_t, z_t, ACT.Relu).then_inc(z_relu, 1)

            def normalise(m, j):
                t = number(m, j)
                act.wait_ge(f_coef, t + 1)
                wait(act, xT_ps, t)
                act.activation(x1n_t, x1_t[:, j, :], ACT.Identity, bias=f_bi[:, j, :],
                               scale=f_sc[:, j, :]).then_inc(x1n_ready, 1)

            def transposed(m, j):
                t = number(m, j)
                act.wait_ge(xT_ps, t + 1)
                wait(act, h_ps, t)
                act.copy(xt_t, ps_t[:, :]).then_inc(xT_ready, 1)

            def hidden(m, j):
                t = number(m, j)
                act.wait_ge(h_ps, t + 1)
                wait(act, h_ready, t * 2)
                act.activation(h_t[:, :], ps_t[:, 0:P], ACT.Gelu_apprx_tanh, bias=b1_t[:, :],
                               scale=1.0).then_inc(h_gelu, 1)

            def hidden_high(m, j):
                t = number(m, j)
                act.wait_ge(h_gelu, t + 1)
                wait(act, q_ps, t)
                act.copy(h_a[:, :], h_t[:, :]).then_inc(h_hi, 1)
                act.copy(h_b[0:FF, :], h_t[0:FF, :]).then_inc(h_ready, 1)

            def step(m, j):
                for shift, what in ((-2, hidden), (-2, hidden_high), (1, high_part), (-1, normalise), (2, high_rows),
                                    (-1, transposed), (2, own_rows), (0, relu)):
                    tm, tj = tile(m, j, shift)
                    if exists(tm, tj):
                        what(tm, tj)

            act.wait_ge(b_in, 48)
            act.wait_ge(g_zero, 3)
            steps(act, step)

        @block.vector
        def _(dve):
            n = 0

            def chain(ins):
                nonlocal n
                n += 1
                ins.then_inc(prep, 1)
                dve.wait_ge(prep, n)

            def inverse_root(v, a, y, result, link):
                link(dve.tensor_scalar(a.bitcast(I32), v.bitcast(I32), 1, None, ALU.arith_shift_right))
                link(dve.tensor_scalar(y.bitcast(I32), a.bitcast(I32), -1.0, float(0x5F3759DF), ALU.mult, ALU.add))
                c = 1.0
                for _ in range(3):
                    if y.shape[1] == 1:
                        link(dve.scalar_tensor_tensor(a, y, y, v, ALU.mult, ALU.mult))
                    else:
                        link(dve.tensor_tensor(a, y, y, ALU.mult))
                        link(dve.tensor_tensor(a, a, v, ALU.mult))
                    link(dve.scalar_tensor_tensor(y, a, 3.0 * c * c, y, ALU.subtract, ALU.mult))
                    c = -2.0 * c ** 3
                link(dve.tensor_scalar(result, y, 1.0 / c, None, ALU.mult))

            e = slice(0, EP)
            dve.wait_ge(dst_in, 16)
            dve.wait_ge(src_in, 16)
            dve.tensor_scalar(tile_i[e, :], dst_i[e, :], 7, None, ALU.arith_shift_right)
            dve.tensor_scalar(low_i[e, :], dst_i[e, :], P - 1, None, ALU.bitwise_and)
            dve.tensor_scalar(shi_e[e, :], src_i[e, 0:EC], 7, None, ALU.arith_shift_right)
            dve.tensor_scalar(didx_e[e, 0:EC], src_i[e, 0:EC], P - 1, None, ALU.bitwise_and)
            dve.tensor_scalar(top_i[e, :], src_i[e, 0:EC], 11, None, ALU.arith_shift_right)
            dve.tensor_scalar(digit_i[e, :], src_i[e, 0:EC], 2047, None, ALU.bitwise_and)
            chain(dve.tensor_tensor(loop_f[e, :], src_i[e, 0:EC], dst_i[e, :], ALU.is_equal))
            dve.tensor_scalar(tile_f[e, :], tile_i[e, :], 0.0, None, ALU.add)
            chain(dve.tensor_scalar(low1[e, :], low_i[e, :], 1.0, None, ALU.add))
            dve.scalar_tensor_tensor(didx_e[e, 0:EC], didx_e[e, 0:EC], float(NT), shi_e[e, :], ALU.mult, ALU.add)
            dve.tensor_copy(src_i[e, EC:EC + 1], src_i[e, 0:1])
            dve.tensor_scalar(digit1[e, :], digit_i[e, :], 0.0, None, ALU.add)
            dve.scalar_tensor_tensor(digit2[e, :], top_i[e, :], 256.0, low1[e, :], ALU.mult,
                                     ALU.add).then_inc(digits_ready, 1)
            dve.scalar_tensor_tensor(tile_lp[e, :], loop_f[e, :], BIG, tile_f[e, :], ALU.mult,
                                     ALU.add)
            chain(dve.scalar_tensor_tensor(tile_nb[e, :], loop_f[e, :], -BIG, tile_f[e, :], ALU.mult, ALU.add))
            dve.tensor_copy(didx_e[e, EC:EC + 1], didx_e[e, 0:1])
            dve.wait_ge(consts, 5)
            dve.tensor_tensor(in_tile3[e], iota_t[e, :, None].to_broadcast([EP, NT, EC]),
                              tile_nb[e, None, :].to_broadcast([EP, NT, EC]), ALU.is_equal).then_inc(tiles_ready, 1)
            dve.wait_ge(tiles_ready, 1)
            dve.wait_ge(uv2_ps, 1)
            dve.tensor_copy(count, in_tile[e, :]).then_inc(count_in, 1)
            dve.wait_ge(base_ready, 1)
            chain(dve.tensor_reduce(base_t[:, :], ps_a[:, 0:NT * GROUP].rearrange("p (t g) -> p t g", g=GROUP), AX.X, ALU.add))
            dve.tensor_scalar(base_t[:, :], base_t[:, :], 1024.0, None, ALU.min).then_inc(count_in, 1)
            dve.wait_ge(count_in, 2)
            chain(dve.tensor_tensor(count3[:, :, 0:1], count3[:, :, 0:1], base_t[e, :, None], ALU.add))
            dve.wait_ge(mask_ready, 2)
            dve.tensor_tensor_scan(count, not_first, count, 0.0, ALU.mult, ALU.add).then_inc(scanned, 1)
            dve.wait_ge(scanned, 1)
            chain(dve.tensor_tensor(count, count, in_tile[e, :], ALU.mult))
            left = NT
            while left > 1:
                low, left = left // 2, (left + 1) // 2
                chain(dve.tensor_tensor(count[:, 0:low * EC], count[:, 0:low * EC],
                                        count[:, left * EC:(left + low) * EC], ALU.add))
            dve.memset(most[:, :], 0.0)
            chain(dve.tensor_copy(rank1[e, :], count[:, 0:EC]))
            dve.tensor_reduce(most[e, :], rank1[e, :], AX.X, ALU.max).then_inc(most_ready, 1)
            dve.wait_ge(uv_ready, 5)
            dve.tensor_tensor(uv2_b[0:FF, :], ps_q[0:FF, :], uv2_a[0:FF, :].bitcast(F32),
                              ALU.subtract).then_inc(uv2_part, 1)
            dve.tensor_tensor(uv2_b[96:97, :], b2_t[96:97, :], uv2_b[96:97, :].bitcast(F32),
                              ALU.subtract).then_inc(uv2_part, 1)

            dve.wait_ge(w_lo_ready, KC)

            def slot_rows(q):
                for r in range(2):
                    g = q * 2 + r
                    wait(dve, slot_val_ready, g * 2 - 2)
                    dve.tensor_tensor(slot_hot[e, r], iota_16[e, None, 0:SLOTS].to_broadcast([EP, GROUP, SLOTS]),
                                      rank1[e, bass.ds(g * GROUP, GROUP), None].to_broadcast([EP, GROUP, SLOTS]),
                                      ALU.is_equal).then_inc(slot_ready, 1)

            def hot_rows(q):
                for r in range(2):
                    g = q * 2 + r
                    wait(dve, hot_used, g - 1)
                    for rows, iota, value in ((node_hot, iota_16, low1), (loop_hot, iota_self, tile_lp)):
                        width = iota.shape[1]
                        dve.tensor_tensor(rows[e, r], iota[e, None, :].to_broadcast([EP, GROUP, width]),
                                          value[e, bass.ds(g * GROUP, GROUP), None].to_broadcast([EP, GROUP, width]),
                                          ALU.is_equal).then_inc(hot_ready, 1)

            slot_rows(0)
            hot_rows(0)
            with dve.Fori(1, EC // (2 * GROUP)) as q:
                slot_rows(q)
                hot_rows(q)
            dve.wait_ge(hot_used, EC // GROUP)
            chain(dve.tensor_scalar(loops1[:, :], ps_z[:, H2:H2 + NT], 1.0, None, ALU.add))
            chain(dve.tensor_tensor(deg[:, :], loops1[:, :], ps_z[:, 0:NT], ALU.add))
            inverse_root(deg[:, :], dinv_a[:, :], dinv_y[:, :], dinv[:, :], chain)
            chain(dve.tensor_tensor(dinv2[:, :], dinv[:, :], dinv[:, :], ALU.mult))
            dve.tensor_tensor(own[:, :], dinv2[:, :], loops1[:, :], ALU.mult).then_inc(prep, 1)
            n += 1
            dve.wait_ge(slot_used, EC // GROUP)
            dve.tensor_copy(tq[:, :], ps_a[:, H2:H2 + NT]).then_inc(tq_ready, 1)
            dve.wait_ge(digits_ps, 1)
            first, second = ps_t[:, 0:NT], ps_t[:, H2:H2 + NT]
            dve.tensor_scalar(empty[:, :], second, 0.0, float(1 << 20), ALU.is_equal, ALU.mult)
            chain(dve.tensor_scalar(code_i[:, :], second, 0.0, None, ALU.add))
            dve.tensor_scalar(nb_hi[:, :], code_i[:, :], 8, None, ALU.arith_shift_right)
            chain(dve.tensor_scalar(nb_lo[:, :], code_i[:, :], 255, None, ALU.bitwise_and))
            dve.tensor_scalar(nb_row[:, :], nb_lo[:, :], 0.0, None, ALU.add)
            chain(dve.scalar_tensor_tensor(nb_from[:, :], nb_hi[:, :], 2048.0, first, ALU.mult, ALU.add))
            dve.tensor_tensor(nb_src[:, :], nb_from[:, :], empty[:, :], ALU.add)
            dve.tensor_scalar(nb_hi[:, :], nb_from[:, :], 7, None, ALU.arith_shift_right)
            chain(dve.tensor_scalar(nb_lo[:, :], nb_from[:, :], P - 1, None, ALU.bitwise_and))
            dve.scalar_tensor_tensor(nb_didx[:, :], nb_lo[:, :], float(NT), nb_hi[:, :], ALU.mult,
                                     ALU.add).then_inc(tables_ready, 1)
            dve.wait_ge(tables_ready, 1)
            dve.wait_ge(most_ps, 1)
            chain(dve.tensor_reduce(most_row[:, :], ps_q[0:1, 0:P], AX.X, ALU.max))
            dve.tensor_scalar(over_i[:, :], most_row[:, :], float(SLOTS), None, ALU.is_gt).then_inc(over_ready, 1)
            dve.wait_ge(b_in, 48)

            def links(s, start):
                done = [0]

                def link(ins):
                    done[0] += 1
                    ins.then_inc(s, 1)
                    dve.wait_ge(s, start + done[0])
                return link

            def coefs(m, j):
                t = number(m, j)
                link = links(coef_link, t * 16)
                dve.wait_ge(x_in[j], m * 16 + 16)
                for h in range(2):
                    dve.bn_stats(ag_st[:, 0, h, :], x_t[:, j, h * H2:(h + 1) * H2])
                dve.wait_ge(g_in[j], m * 16 + 16)
                dve.bn_stats(ag_st[:, 1, 0, :], g_t[:, j, 0:H2])
                wait(dve, nb_sum, t - B + 1)
                link(dve.bn_stats(ag_st[:, 1, 1, :], g_t[:, j, H2:D]))
                dve.tensor_scalar(spread[:, j, :], iota_1[:, :], nb_row[:, bass.ds(t, 1)], None,
                                  ALU.is_equal).then_inc(spread_ready, 1)
                dve.bn_aggr(ag_mv[:, 0, :], ag_st[:, 0, :, :])
                link(dve.bn_aggr(ag_mv[:, 1, :], ag_st[:, 1, :, :]))
                link(dve.tensor_scalar(ag_v[:, :], ag_mv[:, :, 1], EPS, None, ALU.add))
                inverse_root(ag_v[:, :], ag_a[:, :], ag_y[:, :], ag_v[:, :], link)
                dve.wait_ge(d_in[j], m * 16 + 16)
                dve.tensor_scalar(x_sc[:, j, :], ag_v[:, 0:1], own[:, bass.ds(t, 1)], None, ALU.mult)
                link(dve.tensor_scalar(g_sc[:, j, :], ag_v[:, 1:2], g_dinv[:, j:j + 1], None, ALU.mult))
                dve.scalar_tensor_tensor(x_bi[:, j, :], ag_mv[:, 0, 0:1], -1.0, x_sc[:, j, :], ALU.mult,
                                         ALU.mult).then_inc(x_coef, 1)
                dve.scalar_tensor_tensor(g_bi[:, j, :], ag_mv[:, 1, 0:1], -1.0, g_sc[:, j, :], ALU.mult,
                                         ALU.mult).then_inc(g_coef, 1)

            def neighbour_rows(m, j):
                t = number(m, j)
                dve.wait_ge(g_coef, t + 1)
                wait(dve, gn_lo, t)
                dve.tensor_scalar(gn_t, g_t[:, j, :], g_sc[:, j, :], g_bi[:, j, :], ALU.mult,
                                  ALU.add).then_inc(gn_ready, 1)

            def hidden_low(m, j):
                t = number(m, j)
                dve.wait_ge(h_hi, t + 1)
                dve.tensor_tensor(h_a[FF:P, :], h_t[FF:P, :], h_a[FF:P, :].bitcast(F32),
                                  ALU.subtract).then_inc(h_ready, 1)

            def add_bias(m, j):
                t = number(m, j)
                dve.wait_ge(z_ps, t + 1)
                wait(dve, x1_ready, t)
                dve.tensor_tensor(z_t, ps_z[:, :], b_all, ALU.add).then_inc(z_biased, 1)

            def mix(m, j, over):
                t = number(m, j)
                dve.wait_ge(nb_sum, t + 1)
                if over:
                    dve.wait_ge(o_used, t * EC + EC + 1)
                dve.wait_ge(xs_ready, t + 1)
                wait(dve, yT_ps, t)
                dve.scalar_tensor_tensor(y_t, ps_a[:, :], dinv[:, bass.ds(t, 1)], xs_t, ALU.mult,
                                         ALU.add).then_inc(y_ready, 1)

            def low_part(m, j):
                t = number(m, j)
                dve.wait_ge(yT_hi, t + 1)
                dve.tensor_tensor(yt_lo[:, j, :], ps_t[:, :], yt_hi[:, j, :].bitcast(F32),
                                  ALU.subtract).then_inc(yT_lo, 1)

            def ffn_stats(m, j):
                t = number(m, j)
                dve.wait_ge(x1_ready, t + 1)
                dve.bn_stats(f_st[:, 0, :], x1_t[:, j, 0:H2])
                dve.bn_stats(f_st[:, 1, :], x1_t[:, j, H2:D]).then_inc(f_stats, 1)
                dve.wait_ge(f_stats, t + 1)

            def ffn_coef(m, j):
                t = number(m, j)
                link = links(f_link, t * 11)
                link(dve.bn_aggr(f_mv[:, :], f_st[:, :, :]))
                link(dve.tensor_scalar(f_v[:, :], f_mv[:, 1:2], EPS, None, ALU.add))
                inverse_root(f_v[:, :], f_a[:, :], f_y[:, :], f_sc[:, j, :], link)
                dve.scalar_tensor_tensor(f_bi[:, j, :], f_mv[:, 0:1], -1.0, f_sc[:, j, :], ALU.mult,
                                         ALU.mult).then_inc(f_coef, 1)

            def result(m, j):
                t = number(m, j)
                dve.wait_ge(q_ps, t + 1)
                dve.wait_ge(x1n_ready, t + 1)
                dve.tensor_tensor(x1_t[:, j, :], ps_q[:, :], x1_t[:, j, :], ALU.add).then_inc(out_ready, 1)

            def general(m, j):
                t = number(m, j)
                with dve.Fori(0, EC) as c:
                    k = t * EC + c
                    link = links(o_chain, k * 15)
                    dve.wait_ge(o_used, k + 1)
                    dve.wait_ge(o_in, k * 16 + 16)
                    dve.wait_ge(o_din, k * 16 + 16)
                    dve.bn_stats(o_st[e, 0, :], og_t[e, 0:H2])
                    link(dve.bn_stats(o_st[e, 1, :], og_t[e, H2:D]))
                    link(dve.tensor_scalar(o_late[e, :], rank1[e, bass.ds(c, 1)], float(SLOTS), None, ALU.is_gt))
                    dve.scalar_tensor_tensor(o_mine[e, :], tile_nb[e, bass.ds(c, 1)], iota_t[e, bass.ds(t, 1)],
                                             o_late[e, :], ALU.is_equal, ALU.mult)
                    link(dve.bn_aggr(o_mv[e, :], o_st[e, :, :]))
                    link(dve.tensor_scalar(o_v[e, :], o_mv[e, 1:2], EPS, None, ALU.add))
                    inverse_root(o_v[e, :], o_a[e, :], o_y[e, :], o_v[e, :], link)
                    link(dve.tensor_scalar(o_sc[e, :], o_v[e, :], o_dinv[e, :], None, ALU.mult))
                    link(dve.tensor_scalar(on_t[e, :], og_t[e, :], o_mv[e, 0:1], o_sc[e, :], ALU.subtract, ALU.mult))
                    dve.tensor_scalar(o_hot[e, :], iota_1[e, :], low1[e, bass.ds(c, 1)], o_mine[e, :],
                                      ALU.is_equal, ALU.mult).then_inc(o_ready, 1)

            def main(over):
                def step(m, j):
                    tm, tj = tile(m, j, 1)
                    if exists(tm, tj):
                        if over:
                            general(tm, tj)
                        mix(tm, tj, over)
                    for shift, what in ((-1, ffn_stats), (-2, hidden_low), (-1, ffn_coef), (1, low_part), (2, coefs),
                                        (2, neighbour_rows), (-2, result), (0, add_bias)):
                        tm, tj = tile(m, j, shift)
                        if exists(tm, tj):
                            what(tm, tj)

                if over:
                    dve.sem_inc(o_ready, 1)
                steps(dve, step)

            dve.wait_ge(over_ready, 1)
            over = dve.value_load(over_i[0:1, 0:1], min_val=0, max_val=1)
            with dve.If(over > 0):
                main(True)
            with dve.Else():
                main(False)

        @block.tensor
        def _(pe):
            pe.wait_ge(ident_ready, 4)
            pe.wait_ge(u_in, 64)
            for r in range(RC):
                for k in range(KC):
                    mm = pe.transpose((ps_t, ps_q)[r][:, k * P:(k + 1) * P], u1_t[:, k, r * P:(r + 1) * P], ident[:, :])
            mm.then_inc(u1T_ps, 1)
            for r in range(RC):
                mm = pe.transpose(ps_z[:, r * FF:(r + 1) * FF], u2_t[0:FF, r * P:(r + 1) * P], ident[0:FF, 0:FF])
            mm.then_inc(u2T_ps, 1)
            pe.wait_ge(tiles_ready, 1)
            for g in range(EC // GROUP):
                mm = pe.matmul(ps_a[:, 0:NT * GROUP], below[0:EP, :], in_tile3[0:EP, :, g * GROUP:(g + 1) * GROUP],
                               start=(g == 0), stop=(g == EC // GROUP - 1))
            mm.then_inc(base_ready, 1)
            pe.wait_ge(u1T_sb, 2)
            for k in range(KC):
                for r in range(RC):
                    mm = pe.matmul(ps_t[:, k * FF:(k + 1) * FF], u1T[:, r, k * P:(k + 1) * P], v1_t[:, r, :],
                                   start=(r == 0), stop=(r == RC - 1))
            mm.then_inc(uv1_ps, 1)
            pe.wait_ge(u2T_sb, 2)
            for h in range(2):
                for r in range(RC):
                    mm = pe.matmul(ps_q[:, h * H2:(h + 1) * H2], u2T[:, r], v2_t[:, r, h * H2:(h + 1) * H2],
                                   start=(r == 0), stop=(r == RC - 1))
            mm.then_inc(uv2_ps, 1)
            def turns(turn):
                turn(0)
                with pe.Fori(1, EC // (2 * GROUP) - 1) as q:
                    turn(q)
                turn(EC // (2 * GROUP) - 1)

            def is_at(c, value):
                return isinstance(c, int) and c == value

            def degrees(q):
                for r in range(2):
                    g = q * 2 + r
                    pe.wait_ge(hot_ready, g * 2 + 2)
                    for k in range(GROUP):
                        c = g * GROUP + k
                        pe.matmul(ps_z[:, 0:NT], node_hot[0:EP, r, k, :], in_tile3[0:EP, :, bass.ds(c, 1)],
                                  start=is_at(c, 0), stop=is_at(c, EC - 1))
                        mm = pe.matmul(ps_z[:, H2:H2 + NT], node_hot[0:EP, r, k, :], loop_hot[0:EP, r, k, :],
                                       start=is_at(c, 0), stop=is_at(c, EC - 1))
                    mm.then_inc(hot_used, 1)

            def slots(q):
                for r in range(2):
                    g = q * 2 + r
                    pe.wait_ge(slot_val_ready, g * 2 + 2)
                    for k in range(GROUP):
                        c = g * GROUP + k
                        mm = pe.matmul(ps_a[:, H2:H2 + NT], slot_val[0:EP, r, k], in_tile3[0:EP, :, bass.ds(c, 1)],
                                       start=is_at(c, 0), stop=is_at(c, EC - 1))
                    mm.then_inc(slot_used, 1)

            def both(q):
                degrees(q)
                slots(q)

            turns(both)
            pe.wait_ge(tq_ready, 1)
            pe.wait_ge(uv_ready, 3)
            for bank, digit in enumerate((ident[:, 0:SLOTS], ident[:, SLOTS:P])):
                for half in range(2):
                    mm = pe.matmul(ps_t[half * SLOTS:(half + 1) * SLOTS, bank * H2:bank * H2 + NT], digit, tq[:, :],
                                   start=True, stop=True)
            mm.then_inc(digits_ps, 1)
            pe.wait_ge(most_ready, 1)
            pe.wait_ge(uv2_part, 2)
            pe.transpose(ps_q[0:1, 0:P], most[:, :], ident[:, :]).then_inc(most_ps, 1)
            pe.wait_ge(w_hi_ready, KC)
            pe.wait_ge(w_lo_ready, KC)

            def neighbours(m, j):
                t = number(m, j)
                pe.wait_ge(gn_lo, t + 1)
                pe.wait_ge(spread_ready, t + 1)
                wait(pe, y_ready, t)
                for h in range(2):
                    mm = pe.matmul(ps_a[:, h * H2:(h + 1) * H2], spread[:, j, :], gn_r[:, h * H2:(h + 1) * H2],
                                   start=True, stop=True)
                mm.then_inc(nb_sum, 1)

            def general(m, j):
                t = number(m, j)
                with pe.Fori(0, EC) as c:
                    pe.wait_ge(o_ready, t * EC + c + 2)
                    for h in range(2):
                        mm = pe.matmul(ps_a[:, h * H2:(h + 1) * H2], o_hot[0:EP, :], on_t[0:EP, h * H2:(h + 1) * H2],
                                       start=False, stop=True, skip_group_check=True)
                    mm.then_inc(o_used, 1)

            def product(m, j, part):
                t = number(m, j)
                if part == 0:
                    pe.wait_ge(yT_lo, t + 1)
                    wait(pe, z_biased, t)
                for k in range(part * KC // 4, (part + 1) * KC // 4):
                    lhs_hi, lhs_lo = yt_hi[:, j, k * P:(k + 1) * P], yt_lo[:, j, k * P:(k + 1) * P]
                    for a, w in ((lhs_hi, w_hi), (lhs_hi, w_lo), (lhs_lo, w_hi)):
                        for h in range(2):
                            mm = pe.matmul(ps_z[:, h * H2:(h + 1) * H2], a, w[:, k, h * H2:(h + 1) * H2],
                                           start=(k == 0 and a is lhs_hi and w is w_hi),
                                           stop=(k == KC - 1 and a is lhs_lo))
                if part == 3:
                    mm.then_inc(z_ps, 1)

            def turn_y(m, j):
                t = number(m, j)
                pe.wait_ge(y_ready, t + 1)
                wait(pe, h_gelu, t - 2)
                for k in range(KC):
                    mm = pe.transpose(ps_t[:, k * P:(k + 1) * P], y_t[:, k * P:(k + 1) * P], ident[:, :])
                mm.then_inc(yT_ps, 1)

            def turn_x(m, j):
                t = number(m, j)
                pe.wait_ge(x1n_ready, t + 1)
                if isinstance(m, int):
                    wait(pe, yT_lo, min(t + 3, NT))
                else:
                    pe.wait_ge(yT_lo, t + 3)
                for k in range(KC):
                    mm = pe.transpose(ps_t[:, k * P:(k + 1) * P], x1n_t[:, k * P:(k + 1) * P], ident[:, :])
                mm.then_inc(xT_ps, 1)

            def ffn_in(m, j):
                t = number(m, j)
                pe.wait_ge(xT_ready, t + 1)
                for k in range(KC):
                    mm = pe.matmul(ps_t[:, 0:P], uv1[:, k], xt_t[:, k * P:(k + 1) * P],
                                   start=(k == 0), stop=(k == KC - 1))
                mm.then_inc(h_ps, 1)

            def ffn_out(m, j):
                t = number(m, j)
                pe.wait_ge(h_ready, t * 2 + 2)
                wait(pe, out_ready, t)
                for h in range(2):
                    cols = slice(h * H2, (h + 1) * H2)
                    pe.matmul(ps_q[:, cols], h_a[:, :], uv2_a[:, cols], start=True, stop=False)
                    mm = pe.matmul(ps_q[:, cols], h_b[:, :], uv2_b[:, cols], start=False, stop=True)
                mm.then_inc(q_ps, 1)

            def main(over):
                def step(m, j):
                    now, after, before, past = (m, j), tile(m, j, 1), tile(m, j, -1), tile(m, j, -2)
                    if exists(*after):
                        neighbours(*after)
                        if over:
                            general(*after)
                    if exists(*now):
                        product(*now, 0)
                    if exists(*after):
                        turn_y(*after)
                    if exists(*now):
                        product(*now, 1)
                    if exists(*past):
                        ffn_out(*past)
                    if exists(*now):
                        product(*now, 2)
                    if exists(*before):
                        turn_x(*before)
                    if exists(*now):
                        product(*now, 3)
                    if exists(*before):
                        ffn_in(*before)

                steps(pe, step)

            pe.wait_ge(over_ready, 1)
            over = pe.value_load(over_i[0:1, 0:1], min_val=0, max_val=1)
            with pe.If(over > 0):
                main(True)
            with pe.Else():
                main(False)


_INS = ["x", "src", "dst", "L0_gnn_W", "L0_gnn_b", "L0_ffn_U1", "L0_ffn_V1", "L0_ffn_b1", "L0_ffn_U2", "L0_ffn_V2",
        "L0_ffn_b2"]


def kernel(**inputs):
    import numpy as np
    import concourse.bacc as bacc
    from concourse.bass_utils import run_bass_kernel_spmd

    nc = bacc.Bacc("TRN2", target_bir_lowering=False, num_devices=1)
    arrays, args = {}, []
    for name in _INS:
        a = np.ascontiguousarray(inputs[name])
        arrays[f"in_{name}"] = a
        args.append(nc.dram_tensor(f"in_{name}", a.shape, mybir.dt.from_np(a.dtype), kind="ExternalInput").ap())
    out = nc.dram_tensor("out", inputs["x"].shape, mybir.dt.float32, kind="ExternalOutput").ap()
    gcn_ffn(nc, *args, out)
    r = run_bass_kernel_spmd(nc, [arrays], core_ids=[0])
    return r.results[0]["out"]
```

```python
from contextlib import ExitStack

import concourse.bass as bass
from concourse import mybir



def gcn_ffn(nc, x, src, dst, W, b, U1, V1, b1, U2, V2, b2, out):
    F32, F32R, F16, I32 = mybir.dt.float32, mybir.dt.float32r, mybir.dt.float16, mybir.dt.int32
    ALU = mybir.AluOpType
    ACT = mybir.ActivationFunctionType
    AX = mybir.AxisListType

    P = 128
    N, D = x.shape
    E = src.shape[0]
    RANK, FF = V1.shape
    EPS = 1e-5
    NT = (N + P - 1) // P
    LAST = N - (NT - 1) * P
    EP = max(p for p in range(1, P + 1) if E % p == 0)
    EC = E // EP
    KC = D // P
    RC = RANK // P
    H2 = D // 2
    SLOTS = P // 2
    WB = 4
    B = 4
    YB = 2
    BIG = 1000.0
    ROOT = -256.0 / 3.0
    LINKS = 9
    GROUP = 5
    assert EC % (2 * GROUP) == 0 and EC >= 4 * GROUP and GROUP * NT <= H2 and N <= 7 * 2048 and D == 1024 and FF <= 64 and H2 == 512

    ctx = ExitStack()
    with ctx:
        def sb(name, shape, dt):
            return ctx.enter_context(nc.sbuf_tensor(name, shape, dt))

        def sem(name):
            return ctx.enter_context(nc.semaphore(name))

        w_hi = sb("w_hi", [P, KC, D], F32R)
        w_lo = sb("w_lo", [P, KC, D], F32R)
        yt_hi = sb("yt_hi", [P, YB, D], F32R)
        yt_lo = sb("yt_lo", [P, YB, D], F32R)
        in_tile = sb("in_tile", [P, max(NT * EC, 6 * D)], F16)
        gn_hi_t = in_tile[:, 0:2 * D].bitcast(F32R)
        in_tile3 = in_tile[:, 0:NT * EC].rearrange("p (t c) -> p t c", c=EC)

        shared = sb("shared", [P, 19 * D], F32)
        g_t = shared[:, 0:4 * D].rearrange("p (b d) -> p b d", b=B)
        x_t = shared[:, 4 * D:8 * D].rearrange("p (b d) -> p b d", b=B)
        xs_t = shared[:, 8 * D:9 * D]
        y_t = shared[:, 9 * D:10 * D]
        x1n_t = shared[:, 10 * D:11 * D]
        xt_t = shared[:, 11 * D:12 * D]
        x1_t = shared[:, 12 * D:16 * D].rearrange("p (b d) -> p b d", b=B)
        z_t = shared[:, 16 * D:17 * D]
        b_all = shared[:, 17 * D:18 * D]
        gn_t = shared[:, 18 * D:19 * D]
        og_t = in_tile[:, 2 * D:4 * D].bitcast(F32)
        on_t = in_tile[:, 4 * D:6 * D].bitcast(F32)
        not_first = shared[:, 0:4 * D].bitcast(F16)[0:EP, 0:NT * EC]
        count = shared[:, 4 * D:8 * D].bitcast(F16)[0:EP, 0:NT * EC]
        count3 = count.rearrange("p (t c) -> p t c", c=EC)
        u1T = shared[:, 8 * D:10 * D].rearrange("p (r n) -> p r n", r=RC)
        v2_t = shared[:, 10 * D:12 * D].rearrange("p (r n) -> p r n", r=RC)
        w_stage = shared[:, 12 * D:16 * D].rearrange("p (k n) -> p k n", k=WB)
        hots = shared[:, 8 * D:12 * D].bitcast(F16)
        node_hot = hots[:, 0:2 * GROUP * P].rearrange("p (b g n) -> p b g n", b=2, g=GROUP)
        slot_hot = hots[:, 4 * D:4 * D + 2 * GROUP * SLOTS].rearrange("p (b g n) -> p b g n", b=2, g=GROUP)
        slot_val = hots[:, 5 * D:5 * D + 4 * GROUP * SLOTS].rearrange("p (b g v n) -> p b g v n", b=2, g=GROUP, v=2)
        u1_t = shared[:, 12 * D:14 * D].rearrange("p (k r) -> p k r", k=KC)
        b2_t = shared[:, 18 * D:19 * D]
        SMALL = 16 * D + 14 * EC
        u2_t = shared[:, SMALL:SMALL + RANK]
        v1_t = shared[:, SMALL + RANK:SMALL + RANK + RC * FF].rearrange("p (r f) -> p r f", r=RC)
        u2T = shared[:, SMALL + 384:SMALL + 384 + RC * 2 * FF].rearrange("p (r c f) -> p r c f", r=RC, c=2)
        loop_hot = shared[:, 0:4 * D].bitcast(F16)[0:EP, 0:NT * EC].rearrange("p (g n) -> p g n", g=EC // GROUP)
        edge = [shared[:, 16 * D + i * EC:16 * D + (i + 1) * EC] for i in range(14)]
        tile_i, low_i, shi_e, dst_i, top_i, digit_i = (a.bitcast(I32) for a in edge[0:6])
        tile_f, loop_f = edge[6:8]
        tile_lp = edge[8]
        tile_nb16, low16, rank16, digit1, digit2 = (a.bitcast(F16)[:, 0:EC] for a in edge[9:14])
        assert NT * EC <= 8 * D and 14 * EC + 640 <= 2 * D and KC * RANK <= 2 * D and KC == 8 and RC * D <= 2 * D
        assert RC * FF <= 128 and RANK <= 256 and 4 * GROUP * SLOTS <= 2 * D and 2 * GROUP * P <= 2 * D and FF == 64

        gn_r = sb("gn_r", [P, D], F32R)
        uv1 = sb("uv1", [P, KC, 2, FF], F32)
        uv2_a = sb("uv2_a", [P, D], F32R)
        uv2_b = sb("uv2_b", [P, D], F32R)
        b1_t = sb("b1_t", [P, 1], F32)
        h_t = sb("h_t", [P, P], F32)
        h_a = sb("h_a", [P, P], F32R)
        h_b = sb("h_b", [P, P], F32R)
        tq = sb("tq", [P, NT], F32)
        ident = sb("ident", [P, P], F32)
        below = sb("below", [P, P], F16)
        iota_t = sb("iota_t", [P, NT], F32)
        iota_t16 = sb("iota_t16", [P, NT], F16)
        iota_self = sb("iota_self", [P, NT], F16)
        iota_1 = sb("iota_1", [P, P], F32)
        iota_16 = sb("iota_16", [P, P], F16)
        src_i = sb("src_i", [P, EC + 1], I32)
        didx_e = sb("didx_e", [P, EC + 1], I32)
        low1 = sb("low1", [P, EC], F32)
        tile_nb = sb("tile_nb", [P, EC], F32)
        rank1 = sb("rank1", [P, EC], F32)
        nb_src = sb("nb_src", [P, NT], I32)
        nb_from = sb("nb_from", [P, NT], I32)
        nb_lo = sb("nb_lo", [P, NT], I32)
        nb_hi = sb("nb_hi", [P, NT], I32)
        nb_didx = sb("nb_didx", [P, NT], I32)
        empty = sb("empty", [P, NT], F32)
        nb_row = sb("nb_row", [P, NT], F32)
        loops1 = sb("loops1", [P, NT], F32)
        deg = sb("deg", [P, NT], F32)
        dinv = sb("dinv", [P, NT], F32)
        dinv_a = sb("dinv_a", [P, NT], F32)
        dinv_y = sb("dinv_y", [P, NT], F32)
        dinv2 = sb("dinv2", [P, NT], F32)
        own_sc = sb("own_sc", [P, NT], F32)
        own_bi = sb("own_bi", [P, NT], F32)
        code_i = sb("code_i", [P, NT], I32)
        base_t = sb("base_t", [P, NT], F32)
        most = sb("most", [P, 1], F32)
        most_row = sb("most_row", [1, 1], F32)
        over_i = sb("over_i", [1, 1], I32)
        ln_st = sb("ln_st", [P, 3, 2, 6], F32)
        ln_mv = sb("ln_mv", [P, 3, 2], F32)
        ln_v = sb("ln_v", [P, 3], F32)
        ln_a = sb("ln_a", [P, 3], F32)
        ln_y = sb("ln_y", [P, 3], F32)
        x_sc = sb("x_sc", [P, B, 1], F32)
        x_bi = sb("x_bi", [P, B, 1], F32)
        g_sc = sb("g_sc", [P, B, 1], F32)
        f_sc = sb("f_sc", [P, B, 1], F32)
        f_bi = sb("f_bi", [P, B, 1], F32)
        idx_src = sb("idx_src", [P, B], I32)
        idx_dinv = sb("idx_dinv", [P, B], I32)
        g_dinv = sb("g_dinv", [P, B], F32)
        spread = sb("spread", [P, B, P], F32R)
        o_src = sb("o_src", [P, 2], I32)
        o_didx = sb("o_didx", [P, 2], I32)
        o_dinv = sb("o_dinv", [P, 1], F32)
        o_st = sb("o_st", [P, 2, 6], F32)
        o_mv = sb("o_mv", [P, 2], F32)
        o_v = sb("o_v", [P, 1], F32)
        o_a = sb("o_a", [P, 1], F32)
        o_y = sb("o_y", [P, 1], F32)
        o_sc = sb("o_sc", [P, 1], F32)
        o_late = sb("o_late", [P, 1], F32)
        o_mine = sb("o_mine", [P, 1], F32)
        o_hot = sb("o_hot", [P, P], F32)

        ps_a = ctx.enter_context(nc.psum_tensor("ps_a", [P, D], F32))
        ps_z = ctx.enter_context(nc.psum_tensor("ps_z", [P, D], F32))
        ps_t = ctx.enter_context(nc.psum_tensor("ps_t", [P, D], F32))
        ps_q = ctx.enter_context(nc.psum_tensor("ps_q", [P, D], F32))
        dinv_dram = nc.dram_tensor("dinv_dram", [P * NT, 1], F32, kind="Internal").ap()

        src_in, dst_in, u_in, b_in = sem("src_in"), sem("dst_in"), sem("u_in"), sem("b_in")
        w_in = [sem(f"w_in{k}") for k in range(KC)]
        consts = sem("consts")
        prep = sem("prep")
        tiles_ready = sem("tiles_ready")
        mask_ready = sem("mask_ready")
        ident_ready = sem("ident_ready")
        u1T_ps, u1T_sb, u2T_ps, u2T_sb = sem("u1T_ps"), sem("u1T_sb"), sem("u2T_ps"), sem("u2T_sb")
        uv1_ps, uv2_ps, uv_ready = sem("uv1_ps"), sem("uv2_ps"), sem("uv_ready")
        w_hi_ready, w_lo_ready = sem("w_hi_ready"), sem("w_lo_ready")
        count_in, base_ready = sem("count_in"), sem("base_ready")
        scanned, digits_ready = sem("scanned"), sem("digits_ready")
        b2_in, uv2_part = sem("b2_in"), sem("uv2_part")
        slot_val_ready, loop_dist, loop_ready = sem("slot_val_ready"), sem("loop_dist"), sem("loop_ready")
        tq_ready, digits_ps = sem("tq_ready"), sem("digits_ps")
        hot_ready, hot_used = sem("hot_ready"), sem("hot_used")
        slot_ready, slot_used = sem("slot_ready"), sem("slot_used")
        most_ready, most_ps = sem("most_ready"), sem("most_ps")
        over_ready = sem("over_ready")
        tables_ready = sem("tables_ready")
        dinv_out = sem("dinv_out")
        g_zero = sem("g_zero")
        h_one = sem("h_one")
        gn_hi, gn_lo, h_gelu, h_hi = sem("gn_hi"), sem("gn_lo"), sem("h_gelu"), sem("h_hi")
        x_in = [sem(f"x_in{j}") for j in range(B)]
        g_in = [sem(f"g_in{j}") for j in range(B)]
        d_in = [sem(f"d_in{j}") for j in range(B)]
        out_done = [sem(f"out_done{j}") for j in range(B)]
        idx_ready = sem("idx_ready")
        coef_link = sem("coef_link")
        x_coef, g_coef, f_coef = sem("x_coef"), sem("g_coef"), sem("f_coef")
        spread_ready, gn_ready, xs_ready = sem("spread_ready"), sem("gn_ready"), sem("xs_ready")
        nb_sum, y_ready, yT_ps, yT_hi, yT_lo = (sem(n) for n in ("nb_sum", "y_ready", "yT_ps", "yT_hi", "yT_lo"))
        z_ps, z_biased, z_relu, x1_ready, x1n_ready = (sem(n) for n in ("z_ps", "z_biased", "z_relu", "x1_ready", "x1n_ready"))
        xT_ps, xT_ready, h_ps, h_ready, q_ps, out_ready = (sem(n) for n in ("xT_ps", "xT_ready", "h_ps", "h_ready", "q_ps", "out_ready"))
        o_idx, o_in, o_din, o_chain, o_ready, o_used = (sem(n) for n in ("o_idx", "o_in", "o_din", "o_chain", "o_ready", "o_used"))

        block = ctx.enter_context(nc.Block())

        def tile(m, j, shift):
            j += shift
            return m + j // B, j % B

        def number(m, j):
            return m * B + j

        def steps(eng, step):
            first, last = 2, (NT - 5) // B
            for i in range(-2, B * first):
                step(i // B, i % B)
            with eng.Fori(first, last) as m:
                for j in range(B):
                    step(m, j)
            for i in range(B * last, NT + 2):
                step(i // B, i % B)

        def exists(m, j):
            return not isinstance(m, int) or 0 <= number(m, j) < NT

        def wait(eng, s, value):
            if not isinstance(value, int) or value > 0:
                eng.wait_ge(s, value)

        @block.sync
        def _(sp):
            sp.dma_start(dst_i[0:EP, :], dst.rearrange("(p c) -> p c", p=EP)).then_inc(dst_in, 16)
            sp.dma_start(src_i[0:EP, 0:EC], src.rearrange("(p c) -> p c", p=EP)).then_inc(src_in, 16)
            sp.dma_start(u1_t, U1.rearrange("(k p) r -> p k r", p=P)).then_inc(u_in, 16)
            sp.dma_start(u2_t[0:FF, :], U2).then_inc(u_in, 16)
            sp.dma_start(v1_t, V1.rearrange("(r p) f -> p r f", p=P)).then_inc(u_in, 16)
            sp.dma_start(v2_t, V2.rearrange("(r p) n -> p r n", p=P)).then_inc(u_in, 16)
            for half in range(2):
                sp.dma_start(b1_t[half * FF:(half + 1) * FF, :], b1.rearrange("(f o) -> f o", o=1)).then_inc(b_in, 16)
            for row in (64, 96):
                sp.dma_start(b2_t[row:row + 1, :], b2.rearrange("(o n) -> o n", o=1)).then_inc(b2_in, 16)
            for k in range(KC):
                if k == 2:
                    sp.wait_ge(u1T_ps, 1)
                if k >= WB:
                    sp.wait_ge(w_lo_ready, k - WB + 1)
                sp.dma_start(w_stage[:, (k + 2) % WB, :], W[k * P:(k + 1) * P, :]).then_inc(w_in[k], 16)

            def load(m, j):
                rows = LAST if isinstance(m, int) and number(m, j) == NT - 1 else P
                wait(sp, x1_ready, number(m, j) - B + 1)
                sp.dma_start(x_t[0:rows, j, :], x[bass.ds(number(m, j) * P, rows), :]).then_inc(x_in[j], 16)

            sp.wait_ge(most_ready, 1)
            for t in range(B):
                load(0, t)
            sp.wait_ge(tables_ready, 1)
            sp.dma_start(dinv_dram.rearrange("(p t) o -> p (t o)", p=P), dinv[:, :]).then_inc(dinv_out, 16)
            sp.dma_start(b_all, b.rearrange("(o n) -> o n", o=1).broadcast_to([P, D])).then_inc(b_in, 16)

            def store(m, j):
                rows = LAST if isinstance(m, int) and number(m, j) == NT - 1 else P
                sp.wait_ge(out_ready, number(m, j) + 1)
                sp.dma_start(out[bass.ds(number(m, j) * P, rows), :], x1_t[0:rows, j, :]).then_inc(out_done[j], 16)

            def step(m, j):
                for shift, what in ((-2, store), (3, load)):
                    tm, tj = tile(m, j, shift)
                    if exists(tm, tj) and not (what is load and isinstance(tm, int) and number(tm, tj) < B):
                        what(tm, tj)

            steps(sp, step)
            for j in range(B):
                sp.wait_ge(out_done[j], 16 * len(range(j, NT, B)))
            sp.wait_ge(dinv_out, 16)

        @block.gpsimd
        def _(pool):
            pool.memset(ident[:, :], 0.0).then_inc(ident_ready, 1)
            pool.memset(below[:, :], 0.0).then_inc(ident_ready, 1)
            pool.wait_ge(ident_ready, 2)
            pool.affine_select(out=ident[:, :], in_=ident[:, :], compare_op=ALU.not_equal, fill=1.0, base=0,
                               pattern=[[-1, P]], channel_multiplier=1).then_inc(ident_ready, 1)
            pool.affine_select(out=below[:, :], in_=below[:, :], compare_op=ALU.is_ge, fill=1.0, base=0,
                               pattern=[[-1, P]], channel_multiplier=1).then_inc(ident_ready, 1)
            for table, base in ((iota_t, 0), (iota_t16, 0), (iota_self, int(BIG)), (iota_1, 1), (iota_16, 1)):
                pool.iota(table[:, :], [[1, table.shape[1]]], base=base, channel_multiplier=0,
                          allow_small_or_imprecise_dtypes=True).then_inc(consts, 1)
            pool.memset(not_first, 1.0).then_inc(mask_ready, 1)
            pool.wait_ge(mask_ready, 1)
            pool.memset(not_first.rearrange("p (t c) -> p t c", c=EC)[:, :, 0:1], 0.0).then_inc(mask_ready, 1)
            pool.memset(h_b[:, :].bitcast(F32), 1.0).then_inc(h_one, 1)
            pool.memset(uv2_b[:, :].bitcast(F32), 0.0).then_inc(h_one, 1)
            for k in range(KC):
                pool.wait_ge(w_hi_ready, k + 1)
                pool.tensor_tensor(w_lo[:, k, :], w_stage[:, (k + 2) % WB, :], w_hi[:, k, :].bitcast(F32),
                                   ALU.subtract).then_inc(w_lo_ready, 1)

            def slot_values(q):
                for r in range(2):
                    g = q * 2 + r
                    wait(pool, slot_used, g - 1)
                    pool.wait_ge(slot_ready, g + 1)
                    for v, digit in enumerate((digit1, digit2)):
                        pool.tensor_tensor(slot_val[0:EP, r, :, v, :], slot_hot[0:EP, r],
                                           digit[0:EP, bass.ds(g * GROUP, GROUP), None].to_broadcast([EP, GROUP, SLOTS]),
                                           ALU.mult).then_inc(slot_val_ready, 1)

            slot_values(0)
            with pool.Fori(1, EC // (2 * GROUP)) as q:
                slot_values(q)
            pool.memset(g_dinv[:, :], 0.0).then_inc(g_zero, 1)
            pool.wait_ge(hot_used, EC // GROUP)
            pool.memset(shared[:, 0:B * D], 0.0).then_inc(g_zero, 1)
            pool.wait_ge(tables_ready, 1)
            pool.memset(in_tile[:, 0:2 * D].bitcast(F32), 0.0).then_inc(g_zero, 1)

            last_row = pool.to_reg(N - 1)
            last_dinv = pool.to_reg(P * NT - 1)

            def stage(m, j):
                t = number(m, j)
                wait(pool, g_in[j], m * 16)
                wait(pool, d_in[j], m * 16)
                pool.tensor_copy(idx_src[:, j:j + 1], nb_src[:, bass.ds(t, 1)]).then_inc(idx_ready, 1)
                pool.tensor_copy(idx_dinv[:, j:j + 1], nb_didx[:, bass.ds(t, 1)]).then_inc(idx_ready, 1)

            def gather(m, j):
                t = number(m, j)
                pool.wait_ge(idx_ready, t * 2 + 2)
                wait(pool, gn_ready, t - B + 1)
                if isinstance(m, int) and t == 0:
                    pool.wait_ge(g_zero, 3)
                if exists(*tile(m, j, 1)):
                    stage(*tile(m, j, 1))
                pool.indirect_dma_start(
                    out=g_t[:, j, :], out_offset=None, in_=x,
                    in_offset=bass.IndirectOffsetOnAxis(ap=idx_src[:, j:j + 1], axis=0),
                    bounds_check=last_row, oob_is_err=False).then_inc(g_in[j], 16)
                if isinstance(m, int) and t == 0:
                    pool.wait_ge(dinv_out, 16)
                pool.indirect_dma_start(
                    out=g_dinv[:, j:j + 1], out_offset=None, in_=dinv_dram,
                    in_offset=bass.IndirectOffsetOnAxis(ap=idx_dinv[:, j:j + 1], axis=0),
                    bounds_check=last_dinv, oob_is_err=False).then_inc(d_in[j], 16)

            def low_rows(m, j):
                t = number(m, j)
                pool.wait_ge(gn_ready, t + 1)
                pool.wait_ge(gn_hi, t + 1)
                wait(pool, nb_sum, t)
                pool.tensor_tensor(gn_r[:, :], gn_t, gn_hi_t.bitcast(F32),
                                   ALU.subtract).then_inc(gn_lo, 1)

            def residual(m, j):
                t = number(m, j)
                pool.wait_ge(z_relu, t + 1)
                wait(pool, out_done[j], m * 16)
                pool.tensor_tensor(x1_t[:, j, :], z_t, x_t[:, j, :], ALU.add).then_inc(x1_ready, 1)

            def general(m, j):
                t = number(m, j)
                with pool.Fori(0, EC // 2) as q:
                    for r in range(2):
                        n = t * EC + q * 2 + r
                        pool.wait_ge(o_idx, n * 2 + 2)
                        pool.wait_ge(o_ready, n + 1)
                        stage_edges(q * 2 + r + 1, 1 - r)
                        pool.indirect_dma_start(
                            out=og_t[0:EP, :], out_offset=None, in_=x,
                            in_offset=bass.IndirectOffsetOnAxis(ap=o_src[0:EP, r:r + 1], axis=0),
                            bounds_check=last_row, oob_is_err=False).then_inc(o_in, 16)
                        pool.indirect_dma_start(
                            out=o_dinv[0:EP, :], out_offset=None, in_=dinv_dram,
                            in_offset=bass.IndirectOffsetOnAxis(ap=o_didx[0:EP, r:r + 1], axis=0),
                            bounds_check=last_dinv, oob_is_err=False).then_inc(o_din, 16)

            def stage_edges(c, r):
                pool.tensor_copy(o_src[0:EP, r:r + 1], src_i[0:EP, bass.ds(c, 1)]).then_inc(o_idx, 1)
                pool.tensor_copy(o_didx[0:EP, r:r + 1], didx_e[0:EP, bass.ds(c, 1)]).then_inc(o_idx, 1)

            def main(over):
                stage(0, 0)
                if over:
                    stage_edges(0, 0)
                for t in range(2):
                    gather(0, t)

                def step(m, j):
                    tm, tj = tile(m, j, -1)
                    if exists(tm, tj):
                        residual(tm, tj)
                    tm, tj = tile(m, j, 1)
                    if over and exists(tm, tj):
                        general(tm, tj)
                    tm, tj = tile(m, j, 4)
                    if exists(tm, tj):
                        gather(tm, tj)
                    tm, tj = tile(m, j, 2)
                    if exists(tm, tj):
                        low_rows(tm, tj)

                steps(pool, step)

            pool.wait_ge(over_ready, 1)
            over = pool.value_load(over_i[0:1, 0:1], min_val=0, max_val=1)
            with pool.If(over > 0):
                main(True)
            with pool.Else():
                main(False)

        @block.scalar
        def _(act):
            def split_w(k):
                act.wait_ge(w_in[k], 16)
                act.copy(w_hi[:, k, :], w_stage[:, (k + 2) % WB, :]).then_inc(w_hi_ready, 1)

            for k in range(2):
                split_w(k)
            act.wait_ge(u1T_ps, 1)
            act.copy(u1T[:, 0, :], ps_t[:, :]).then_inc(u1T_sb, 1)
            act.copy(u1T[:, 1, :], ps_q[:, :]).then_inc(u1T_sb, 1)
            act.wait_ge(u2T_ps, 1)
            for c in range(2):
                act.copy(u2T[:, :, c, :], ps_z[:, 0:RC * FF].rearrange("p (r f) -> p r f", r=RC)).then_inc(u2T_sb, 1)
            for k in range(2, 4):
                split_w(k)
            act.wait_ge(uv1_ps, 1)
            for c in range(2):
                act.copy(uv1[:, :, c, :], ps_t[:, 0:KC * FF].rearrange("p (k f) -> p k f", k=KC)).then_inc(uv_ready, 1)
            act.wait_ge(uv2_ps, 1)
            act.copy(uv2_a[:, :], ps_q[:, :]).then_inc(uv_ready, 1)
            act.wait_ge(b2_in, 32)
            act.wait_ge(h_one, 2)
            for row in (64, 96):
                act.copy(uv2_b[row:row + 1, :], b2_t[row:row + 1, :]).then_inc(uv_ready, 1)
            for k in range(4, KC):
                split_w(k)
            act.wait_ge(consts, 5)
            act.wait_ge(digits_ready, 2)
            act.wait_ge(scanned, 1)
            parts = 4
            for part in range(parts):
                first, end = EC // GROUP * part // parts, EC // GROUP * (part + 1) // parts
                with act.Fori(first, end) as g:
                    for k in range(GROUP):
                        dist = act.activation(loop_hot[:, bass.ds(g, 1), k * NT:(k + 1) * NT], iota_self[0:EP, None, :],
                                              ACT.Abs, bias=tile_lp[0:EP, bass.ds(g * GROUP + k, 1)], scale=-1.0)
                    dist.then_inc(loop_dist, 1)
                act.wait_ge(loop_dist, end)
                with act.Fori(first, end) as g:
                    act.activation(loop_hot[:, bass.ds(g, 1), :], loop_hot[:, bass.ds(g, 1), :], ACT.Relu,
                                   bias=iota_1[0:EP, 0:1], scale=-1.0).then_inc(loop_ready, 1)

            def high_rows(m, j):
                t = number(m, j)
                act.wait_ge(gn_ready, t + 1)
                wait(act, gn_lo, t)
                act.copy(gn_hi_t[SLOTS:P, :], gn_t[SLOTS:P, :]).then_inc(gn_hi, 1)

            def own_rows(m, j):
                t = number(m, j)
                act.wait_ge(x_coef, t + 1)
                wait(act, y_ready, t)
                act.activation(xs_t, x_t[:, j, :], ACT.Identity, bias=x_bi[:, j, :],
                               scale=x_sc[:, j, :]).then_inc(xs_ready, 1)

            def high_part(m, j):
                t = number(m, j)
                act.wait_ge(yT_ps, t + 1)
                wait(act, z_ps, (t - YB + 1) * 2)
                act.copy(yt_hi[:, j % YB, :], ps_t[:, :]).then_inc(yT_hi, 1)

            def relu(m, j):
                t = number(m, j)
                act.wait_ge(z_biased, t * 2 + 2)
                act.activation(z_t, z_t, ACT.Relu).then_inc(z_relu, 1)

            def normalise(m, j):
                t = number(m, j)
                act.wait_ge(f_coef, t + 1)
                wait(act, xT_ps, t)
                act.activation(x1n_t, x1_t[:, j, :], ACT.Identity, bias=f_bi[:, j, :],
                               scale=f_sc[:, j, :]).then_inc(x1n_ready, 1)

            def transposed(m, j):
                t = number(m, j)
                act.wait_ge(xT_ps, t + 1)
                wait(act, h_ps, t)
                act.copy(xt_t, ps_t[:, :]).then_inc(xT_ready, 1)

            def hidden(m, j):
                t = number(m, j)
                act.wait_ge(h_ps, t + 1)
                wait(act, h_ready, t * 2)
                act.activation(h_t[:, :], ps_t[:, 0:P], ACT.Gelu_apprx_tanh, bias=b1_t[:, :],
                               scale=1.0).then_inc(h_gelu, 1)

            def hidden_high(m, j):
                t = number(m, j)
                act.wait_ge(h_gelu, t + 1)
                wait(act, q_ps, t)
                act.copy(h_a[:, :], h_t[:, :]).then_inc(h_hi, 1)
                act.copy(h_b[0:FF, :], h_t[0:FF, :]).then_inc(h_ready, 1)

            def step(m, j):
                for shift, what in ((-2, hidden), (-2, hidden_high), (1, high_part), (-1, normalise), (2, high_rows),
                                    (-1, transposed), (2, own_rows), (0, relu)):
                    tm, tj = tile(m, j, shift)
                    if exists(tm, tj):
                        what(tm, tj)

            act.wait_ge(b_in, 48)
            act.wait_ge(g_zero, 3)
            steps(act, step)

        @block.vector
        def _(dve):
            n = 0

            def chain(ins):
                nonlocal n
                n += 1
                ins.then_inc(prep, 1)
                dve.wait_ge(prep, n)

            def inverse_root(v, a, y, link):
                def square():
                    if len(v.shape) == 2 and v.shape[1] <= 3:
                        for c in range(v.shape[1]):
                            ins = dve.scalar_tensor_tensor(a[:, c:c + 1], y[:, c:c + 1], y[:, c:c + 1], v[:, c:c + 1],
                                                           ALU.mult, ALU.mult)
                        link(ins)
                    else:
                        link(dve.tensor_tensor(a, y, y, ALU.mult))
                        link(dve.tensor_tensor(a, a, v, ALU.mult))

                link(dve.tensor_scalar(y.bitcast(I32), v.bitcast(I32), -0.5, float(0x5F3759DF), ALU.mult, ALU.add))
                square()
                link(dve.scalar_tensor_tensor(y, a, 3.0, y, ALU.subtract, ALU.mult))
                square()
                link(dve.scalar_tensor_tensor(a, a, 40.0 / 3.0, a, ALU.subtract, ALU.mult))
                link(dve.scalar_tensor_tensor(y, a, 80.0, y, ALU.add, ALU.mult))

            e = slice(0, EP)
            dve.wait_ge(dst_in, 16)
            dve.wait_ge(src_in, 16)
            dve.tensor_scalar(tile_i[e, :], dst_i[e, :], 7, None, ALU.arith_shift_right)
            dve.tensor_scalar(low_i[e, :], dst_i[e, :], P - 1, None, ALU.bitwise_and)
            dve.tensor_scalar(shi_e[e, :], src_i[e, 0:EC], 7, None, ALU.arith_shift_right)
            dve.tensor_scalar(didx_e[e, 0:EC], src_i[e, 0:EC], P - 1, None, ALU.bitwise_and)
            dve.tensor_scalar(top_i[e, :], src_i[e, 0:EC], 11, None, ALU.arith_shift_right)
            dve.tensor_scalar(digit_i[e, :], src_i[e, 0:EC], 2047, None, ALU.bitwise_and)
            chain(dve.tensor_tensor(loop_f[e, :], src_i[e, 0:EC], dst_i[e, :], ALU.is_equal))
            dve.tensor_scalar(tile_f[e, :], tile_i[e, :], 0.0, None, ALU.add)
            chain(dve.tensor_scalar(low1[e, :], low_i[e, :], 1.0, None, ALU.add))
            dve.scalar_tensor_tensor(didx_e[e, 0:EC], didx_e[e, 0:EC], float(NT), shi_e[e, :], ALU.mult, ALU.add)
            dve.tensor_copy(src_i[e, EC:EC + 1], src_i[e, 0:1])
            dve.tensor_scalar(digit1[e, :], digit_i[e, :], 0.0, None, ALU.add)
            dve.scalar_tensor_tensor(digit2[e, :], top_i[e, :], 256.0, low1[e, :], ALU.mult,
                                     ALU.add).then_inc(digits_ready, 1)
            dve.scalar_tensor_tensor(tile_nb16[e, :], loop_f[e, :], -BIG, tile_f[e, :], ALU.mult, ALU.add)
            chain(dve.scalar_tensor_tensor(tile_nb[e, :], loop_f[e, :], -BIG, tile_f[e, :], ALU.mult, ALU.add))
            dve.wait_ge(consts, 5)
            dve.tensor_tensor(in_tile3[e], iota_t16[e, :, None].to_broadcast([EP, NT, EC]),
                              tile_nb16[e, None, :].to_broadcast([EP, NT, EC]), ALU.is_equal).then_inc(tiles_ready, 1)
            dve.scalar_tensor_tensor(tile_lp[e, :], loop_f[e, :], BIG, tile_f[e, :], ALU.mult, ALU.add)
            dve.tensor_copy(low16[e, :], low1[e, :]).then_inc(digits_ready, 1)
            dve.tensor_copy(didx_e[e, EC:EC + 1], didx_e[e, 0:1])
            dve.wait_ge(tiles_ready, 1)
            dve.tensor_copy(count, in_tile[e, 0:NT * EC]).then_inc(count_in, 1)
            dve.wait_ge(base_ready, 1)
            chain(dve.tensor_reduce(base_t[:, :], ps_a[:, 0:NT * GROUP].rearrange("p (t g) -> p t g", g=GROUP), AX.X, ALU.add))
            dve.tensor_scalar(base_t[:, :], base_t[:, :], 1024.0, None, ALU.min).then_inc(count_in, 1)
            dve.wait_ge(count_in, 2)
            chain(dve.tensor_tensor(count3[:, :, 0:1], count3[:, :, 0:1], base_t[e, :, None], ALU.add))
            dve.wait_ge(mask_ready, 2)
            dve.tensor_tensor_scan(count, not_first, count, 0.0, ALU.mult, ALU.add).then_inc(scanned, 1)
            dve.wait_ge(scanned, 1)
            chain(dve.tensor_tensor(count, count, in_tile[e, 0:NT * EC], ALU.mult))
            left = NT
            while left > 1:
                low, left = left // 2, (left + 1) // 2
                chain(dve.tensor_tensor(count[:, 0:low * EC], count[:, 0:low * EC],
                                        count[:, left * EC:(left + low) * EC], ALU.add))
            dve.memset(most[:, :], 0.0)
            dve.tensor_copy(rank16[e, :], count[:, 0:EC])
            chain(dve.tensor_copy(rank1[e, :], count[:, 0:EC]))
            dve.tensor_reduce(most[e, :], rank1[e, :], AX.X, ALU.max).then_inc(most_ready, 1)
            dve.wait_ge(uv2_ps, 1)

            def slot_rows(q):
                for r in range(2):
                    g = q * 2 + r
                    wait(dve, slot_val_ready, g * 2 - 2)
                    dve.tensor_tensor(slot_hot[e, r], iota_16[e, None, 0:SLOTS].to_broadcast([EP, GROUP, SLOTS]),
                                      rank16[e, bass.ds(g * GROUP, GROUP), None].to_broadcast([EP, GROUP, SLOTS]),
                                      ALU.is_equal).then_inc(slot_ready, 1)

            def hot_rows(q):
                for r in range(2):
                    g = q * 2 + r
                    wait(dve, hot_used, g - 1)
                    dve.tensor_tensor(node_hot[e, r], iota_16[e, None, :].to_broadcast([EP, GROUP, P]),
                                      low16[e, bass.ds(g * GROUP, GROUP), None].to_broadcast([EP, GROUP, P]),
                                      ALU.is_equal).then_inc(hot_ready, 1)

            slot_rows(0)
            hot_rows(0)
            with dve.Fori(1, EC // (2 * GROUP)) as q:
                slot_rows(q)
                hot_rows(q)
            dve.wait_ge(slot_used, EC // GROUP)
            dve.tensor_copy(tq[:, :], ps_a[:, H2:H2 + NT]).then_inc(tq_ready, 1)
            dve.wait_ge(hot_used, EC // GROUP)
            chain(dve.tensor_scalar(loops1[:, :], ps_z[:, H2:H2 + NT], 1.0, None, ALU.add))
            chain(dve.tensor_tensor(deg[:, :], loops1[:, :], ps_z[:, 0:NT], ALU.add))
            inverse_root(deg[:, :], dinv_a[:, :], dinv_y[:, :], chain)
            chain(dve.tensor_scalar(dinv[:, :], dinv_y[:, :], 1.0 / ROOT, None, ALU.mult))
            chain(dve.tensor_tensor(dinv2[:, :], dinv[:, :], dinv[:, :], ALU.mult))
            dve.scalar_tensor_tensor(own_sc[:, :], dinv2[:, :], 1.0 / ROOT, loops1[:, :], ALU.mult, ALU.mult)
            dve.scalar_tensor_tensor(own_bi[:, :], dinv2[:, :], -1.0 / ROOT, loops1[:, :], ALU.mult,
                                     ALU.mult).then_inc(prep, 1)
            n += 1
            dve.wait_ge(digits_ps, 1)
            first, second = ps_t[:, 0:NT], ps_t[:, H2:H2 + NT]
            dve.tensor_scalar(empty[:, :], second, 0.0, float(1 << 20), ALU.is_equal, ALU.mult)
            chain(dve.tensor_scalar(code_i[:, :], second, 0.0, None, ALU.add))
            dve.tensor_scalar(nb_hi[:, :], code_i[:, :], 8, None, ALU.arith_shift_right)
            chain(dve.tensor_scalar(nb_lo[:, :], code_i[:, :], 255, None, ALU.bitwise_and))
            dve.tensor_scalar(nb_row[:, :], nb_lo[:, :], 0.0, None, ALU.add)
            chain(dve.scalar_tensor_tensor(nb_from[:, :], nb_hi[:, :], 2048.0, first, ALU.mult, ALU.add))
            dve.tensor_tensor(nb_src[:, :], nb_from[:, :], empty[:, :], ALU.add)
            dve.tensor_scalar(nb_hi[:, :], nb_from[:, :], 7, None, ALU.arith_shift_right)
            chain(dve.tensor_scalar(nb_lo[:, :], nb_from[:, :], P - 1, None, ALU.bitwise_and))
            dve.scalar_tensor_tensor(nb_didx[:, :], nb_lo[:, :], float(NT), nb_hi[:, :], ALU.mult,
                                     ALU.add).then_inc(tables_ready, 1)
            dve.wait_ge(most_ps, 1)
            chain(dve.tensor_reduce(most_row[:, :], ps_t[0:1, 2 * P:3 * P], AX.X, ALU.max))
            dve.tensor_scalar(over_i[:, :], most_row[:, :], float(SLOTS), None, ALU.is_gt).then_inc(over_ready, 1)
            dve.wait_ge(uv_ready, 4)
            dve.tensor_tensor(uv2_b[0:FF, :], ps_q[0:FF, :], uv2_a[0:FF, :].bitcast(F32),
                              ALU.subtract).then_inc(uv2_part, 1)
            dve.tensor_tensor(uv2_b[96:97, :], b2_t[96:97, :], uv2_b[96:97, :].bitcast(F32),
                              ALU.subtract).then_inc(uv2_part, 1)
            dve.wait_ge(b_in, 48)

            def links(s, start):
                done = [0]

                def link(ins):
                    done[0] += 1
                    ins.then_inc(s, 1)
                    dve.wait_ge(s, start + done[0])
                return link

            def coefs(m, j):
                ft, fj = tile(m, j, -1)
                am, aj = tile(m, j, 2)
                ffn, ahead = exists(ft, fj), exists(am, aj)
                ft, t = number(ft, fj), number(am, aj)
                link = links(coef_link, (number(m, j) + 2) * LINKS)
                which = range(0 if ffn else 1, 3 if ahead else 1)
                cols = slice(which[0], which[-1] + 1)
                if ahead:
                    dve.wait_ge(x_in[aj], am * 16 + 16)
                    for h in range(2):
                        dve.bn_stats(ln_st[:, 1, h, :], x_t[:, aj, h * H2:(h + 1) * H2])
                    dve.wait_ge(g_in[aj], am * 16 + 16)
                    for h in range(2):
                        ins = dve.bn_stats(ln_st[:, 2, h, :], g_t[:, aj, h * H2:(h + 1) * H2])
                if ffn:
                    dve.wait_ge(x1_ready, ft + 1)
                    for h in range(2):
                        ins = dve.bn_stats(ln_st[:, 0, h, :], x1_t[:, fj, h * H2:(h + 1) * H2])
                if ahead:
                    wait(dve, nb_sum, t - B + 1)
                link(ins)
                if ahead:
                    dve.tensor_scalar(spread[:, aj, :], iota_1[:, :], nb_row[:, bass.ds(t, 1)], None,
                                      ALU.is_equal).then_inc(spread_ready, 1)
                for c in which:
                    ins = dve.bn_aggr(ln_mv[:, c, :], ln_st[:, c, :, :])
                link(ins)
                link(dve.tensor_scalar(ln_v[:, cols], ln_mv[:, cols, 1], EPS, None, ALU.add))
                inverse_root(ln_v[:, cols], ln_a[:, cols], ln_y[:, cols], link)
                if ffn:
                    dve.tensor_scalar(f_sc[:, fj, :], ln_y[:, 0:1], 1.0 / ROOT, None, ALU.mult)
                    dve.scalar_tensor_tensor(f_bi[:, fj, :], ln_mv[:, 0, 0:1], -1.0 / ROOT, ln_y[:, 0:1], ALU.mult,
                                             ALU.mult).then_inc(f_coef, 1)
                if ahead:
                    dve.wait_ge(d_in[aj], am * 16 + 16)
                    dve.tensor_scalar(g_sc[:, aj, :], ln_y[:, 2:3], 1.0 / ROOT, g_dinv[:, aj:aj + 1], ALU.mult,
                                      ALU.mult).then_inc(g_coef, 1)
                    dve.tensor_scalar(x_sc[:, aj, :], ln_y[:, 1:2], own_sc[:, bass.ds(t, 1)], None, ALU.mult)
                    dve.scalar_tensor_tensor(x_bi[:, aj, :], ln_mv[:, 1, 0:1], own_bi[:, bass.ds(t, 1)], ln_y[:, 1:2],
                                             ALU.mult, ALU.mult).then_inc(x_coef, 1)

            def neighbour_rows(m, j):
                t = number(m, j)
                dve.wait_ge(g_coef, t + 1)
                wait(dve, gn_lo, t)
                dve.tensor_scalar(gn_t, g_t[:, j, :], ln_mv[:, 2, 0:1], g_sc[:, j, :], ALU.subtract,
                                  ALU.mult).then_inc(gn_ready, 1)

            def hidden_low(m, j):
                t = number(m, j)
                dve.wait_ge(h_hi, t + 1)
                dve.tensor_tensor(h_a[FF:P, :], h_t[FF:P, :], h_a[FF:P, :].bitcast(F32),
                                  ALU.subtract).then_inc(h_ready, 1)

            def add_bias(m, j):
                t = number(m, j)
                wait(dve, x1_ready, t)
                for h in range(2):
                    cols = slice(h * H2, (h + 1) * H2)
                    dve.wait_ge(z_ps, t * 2 + h + 1)
                    dve.tensor_tensor(z_t[:, cols], ps_z[:, cols], b_all[:, cols], ALU.add).then_inc(z_biased, 1)

            def mix(m, j, over):
                t = number(m, j)
                dve.wait_ge(nb_sum, t + 1)
                if over:
                    dve.wait_ge(o_used, t * EC + EC + 1)
                dve.wait_ge(xs_ready, t + 1)
                wait(dve, yT_ps, t)
                dve.scalar_tensor_tensor(y_t, ps_a[:, :], dinv[:, bass.ds(t, 1)], xs_t, ALU.mult,
                                         ALU.add).then_inc(y_ready, 1)

            def low_part(m, j):
                t = number(m, j)
                dve.wait_ge(yT_hi, t + 1)
                dve.tensor_tensor(yt_lo[:, j % YB, :], ps_t[:, :], yt_hi[:, j % YB, :].bitcast(F32),
                                  ALU.subtract).then_inc(yT_lo, 1)

            def result(m, j):
                t = number(m, j)
                dve.wait_ge(q_ps, t + 1)
                dve.wait_ge(x1n_ready, t + 1)
                dve.tensor_tensor(x1_t[:, j, :], ps_q[:, :], x1_t[:, j, :], ALU.add).then_inc(out_ready, 1)

            def general(m, j):
                t = number(m, j)
                with dve.Fori(0, EC) as c:
                    k = t * EC + c
                    link = links(o_chain, k * 12)
                    dve.wait_ge(o_used, k + 1)
                    dve.wait_ge(o_in, k * 16 + 16)
                    dve.wait_ge(o_din, k * 16 + 16)
                    dve.bn_stats(o_st[e, 0, :], og_t[e, 0:H2])
                    link(dve.bn_stats(o_st[e, 1, :], og_t[e, H2:D]))
                    link(dve.tensor_scalar(o_late[e, :], rank1[e, bass.ds(c, 1)], float(SLOTS), None, ALU.is_gt))
                    dve.scalar_tensor_tensor(o_mine[e, :], tile_nb[e, bass.ds(c, 1)], iota_t[e, bass.ds(t, 1)],
                                             o_late[e, :], ALU.is_equal, ALU.mult)
                    link(dve.bn_aggr(o_mv[e, :], o_st[e, :, :]))
                    link(dve.tensor_scalar(o_v[e, :], o_mv[e, 1:2], EPS, None, ALU.add))
                    inverse_root(o_v[e, :], o_a[e, :], o_y[e, :], link)
                    link(dve.tensor_scalar(o_sc[e, :], o_y[e, :], 1.0 / ROOT, o_dinv[e, :], ALU.mult, ALU.mult))
                    link(dve.tensor_scalar(on_t[e, :], og_t[e, :], o_mv[e, 0:1], o_sc[e, :], ALU.subtract, ALU.mult))
                    dve.tensor_scalar(o_hot[e, :], iota_1[e, :], low1[e, bass.ds(c, 1)], o_mine[e, :],
                                      ALU.is_equal, ALU.mult).then_inc(o_ready, 1)

            def main(over):
                def step(m, j):
                    tm, tj = tile(m, j, 1)
                    if exists(tm, tj):
                        if over:
                            general(tm, tj)
                        mix(tm, tj, over)
                    tm, tj = tile(m, j, -2)
                    if exists(tm, tj):
                        hidden_low(tm, tj)
                    if exists(*tile(m, j, -1)) or exists(*tile(m, j, 2)):
                        coefs(m, j)
                    for shift, what in ((1, low_part), (2, neighbour_rows), (-2, result), (0, add_bias)):
                        tm, tj = tile(m, j, shift)
                        if exists(tm, tj):
                            what(tm, tj)

                if over:
                    dve.sem_inc(o_ready, 1)
                steps(dve, step)

            dve.wait_ge(over_ready, 1)
            over = dve.value_load(over_i[0:1, 0:1], min_val=0, max_val=1)
            with dve.If(over > 0):
                main(True)
            with dve.Else():
                main(False)

        @block.tensor
        def _(pe):
            pe.wait_ge(ident_ready, 4)
            pe.wait_ge(u_in, 64)
            for r in range(RC):
                for k in range(KC):
                    mm = pe.transpose((ps_t, ps_q)[r][:, k * P:(k + 1) * P], u1_t[:, k, r * P:(r + 1) * P], ident[:, :])
            mm.then_inc(u1T_ps, 1)
            for r in range(RC):
                mm = pe.transpose(ps_z[:, r * FF:(r + 1) * FF], u2_t[0:FF, r * P:(r + 1) * P], ident[0:FF, 0:FF])
            mm.then_inc(u2T_ps, 1)
            pe.wait_ge(tiles_ready, 1)
            for g in range(EC // GROUP):
                mm = pe.matmul(ps_a[:, 0:NT * GROUP], below[0:EP, :], in_tile3[0:EP, :, g * GROUP:(g + 1) * GROUP],
                               start=(g == 0), stop=(g == EC // GROUP - 1))
            mm.then_inc(base_ready, 1)
            pe.wait_ge(u1T_sb, 2)
            for k in range(KC):
                for r in range(RC):
                    mm = pe.matmul(ps_t[:, k * FF:(k + 1) * FF], u1T[:, r, k * P:(k + 1) * P], v1_t[:, r, :],
                                   start=(r == 0), stop=(r == RC - 1))
            mm.then_inc(uv1_ps, 1)
            pe.wait_ge(u2T_sb, 2)
            for h in range(2):
                for r in range(RC):
                    mm = pe.matmul(ps_q[:, h * H2:(h + 1) * H2], u2T[:, r], v2_t[:, r, h * H2:(h + 1) * H2],
                                   start=(r == 0), stop=(r == RC - 1))
            mm.then_inc(uv2_ps, 1)
            def turns(turn):
                turn(0)
                with pe.Fori(1, EC // (2 * GROUP) - 1) as q:
                    turn(q)
                turn(EC // (2 * GROUP) - 1)

            def is_at(c, value):
                return isinstance(c, int) and c == value

            def degrees(q):
                for r in range(2):
                    g = q * 2 + r
                    pe.wait_ge(hot_ready, g + 1)
                    pe.wait_ge(loop_ready, g + 1)
                    for k in range(GROUP):
                        c = g * GROUP + k
                        pe.matmul(ps_z[:, 0:NT], node_hot[0:EP, r, k, :], in_tile3[0:EP, :, bass.ds(c, 1)],
                                  start=is_at(c, 0), stop=is_at(c, EC - 1))
                        mm = pe.matmul(ps_z[:, H2:H2 + NT], node_hot[0:EP, r, k, :],
                                       loop_hot[:, bass.ds(g, 1), k * NT:(k + 1) * NT],
                                       start=is_at(c, 0), stop=is_at(c, EC - 1))
                    mm.then_inc(hot_used, 1)

            def slots(q):
                for r in range(2):
                    g = q * 2 + r
                    pe.wait_ge(slot_val_ready, g * 2 + 2)
                    for k in range(GROUP):
                        c = g * GROUP + k
                        mm = pe.matmul(ps_a[:, H2:H2 + NT], slot_val[0:EP, r, k], in_tile3[0:EP, :, bass.ds(c, 1)],
                                       start=is_at(c, 0), stop=is_at(c, EC - 1))
                    mm.then_inc(slot_used, 1)

            def both(q):
                degrees(q)
                slots(q)

            turns(both)
            pe.wait_ge(uv_ready, 3)
            pe.wait_ge(most_ready, 1)
            pe.transpose(ps_t[0:1, 2 * P:3 * P], most[:, :], ident[:, :]).then_inc(most_ps, 1)
            pe.wait_ge(tq_ready, 1)
            for bank, digit in enumerate((ident[:, 0:SLOTS], ident[:, SLOTS:P])):
                for half in range(2):
                    mm = pe.matmul(ps_t[half * SLOTS:(half + 1) * SLOTS, bank * H2:bank * H2 + NT], digit, tq[:, :],
                                   start=True, stop=True)
            mm.then_inc(digits_ps, 1)
            pe.wait_ge(w_hi_ready, KC)
            pe.wait_ge(w_lo_ready, KC)

            def neighbours(m, j):
                t = number(m, j)
                pe.wait_ge(gn_lo, t + 1)
                pe.wait_ge(spread_ready, t + 1)
                wait(pe, y_ready, t)
                for h in range(2):
                    mm = pe.matmul(ps_a[:, h * H2:(h + 1) * H2], spread[:, j, :], gn_r[:, h * H2:(h + 1) * H2],
                                   start=True, stop=True)
                mm.then_inc(nb_sum, 1)

            def general(m, j):
                t = number(m, j)
                with pe.Fori(0, EC) as c:
                    pe.wait_ge(o_ready, t * EC + c + 2)
                    for h in range(2):
                        mm = pe.matmul(ps_a[:, h * H2:(h + 1) * H2], o_hot[0:EP, :], on_t[0:EP, h * H2:(h + 1) * H2],
                                       start=False, stop=True, skip_group_check=True)
                    mm.then_inc(o_used, 1)

            def product(m, j, start, stop):
                t = number(m, j)
                order = [(k, h) for k in range(KC - 2) for h in range(2)] + [(k, h) for h in range(2) for k in (KC - 2, KC - 1)]
                products = [(k, h, part) for k, h in order for part in range(3)]
                if start == 0:
                    pe.wait_ge(yT_lo, t + 1)
                    wait(pe, z_biased, t * 2)
                for k, h, part in products[start:stop]:
                    y_part = (yt_hi, yt_hi, yt_lo)[part][:, j % YB, k * P:(k + 1) * P]
                    w_part = (w_hi, w_lo, w_hi)[part][:, k, h * H2:(h + 1) * H2]
                    last = k == KC - 1 and part == 2
                    mm = pe.matmul(ps_z[:, h * H2:(h + 1) * H2], y_part, w_part, start=(k == 0 and part == 0), stop=last)
                    if last:
                        mm.then_inc(z_ps, 1)

            def turn_y(m, j):
                t = number(m, j)
                pe.wait_ge(y_ready, t + 1)
                wait(pe, h_gelu, t - 2)
                for k in range(KC):
                    mm = pe.transpose(ps_t[:, k * P:(k + 1) * P], y_t[:, k * P:(k + 1) * P], ident[:, :])
                mm.then_inc(yT_ps, 1)

            def turn_x(m, j):
                t = number(m, j)
                pe.wait_ge(x1n_ready, t + 1)
                if isinstance(m, int):
                    wait(pe, yT_lo, min(t + 3, NT))
                else:
                    pe.wait_ge(yT_lo, t + 3)
                for k in range(KC):
                    mm = pe.transpose(ps_t[:, k * P:(k + 1) * P], x1n_t[:, k * P:(k + 1) * P], ident[:, :])
                mm.then_inc(xT_ps, 1)

            def ffn_in(m, j):
                t = number(m, j)
                pe.wait_ge(xT_ready, t + 1)
                for k in range(KC):
                    mm = pe.matmul(ps_t[:, 0:P], uv1[:, k], xt_t[:, k * P:(k + 1) * P],
                                   start=(k == 0), stop=(k == KC - 1))
                mm.then_inc(h_ps, 1)

            def ffn_out(m, j):
                t = number(m, j)
                if isinstance(m, int) and t == 0:
                    pe.wait_ge(uv2_part, 2)
                pe.wait_ge(h_ready, t * 2 + 2)
                wait(pe, out_ready, t)
                for h in range(2):
                    cols = slice(h * H2, (h + 1) * H2)
                    pe.matmul(ps_q[:, cols], h_a[:, :], uv2_a[:, cols], start=True, stop=False)
                    mm = pe.matmul(ps_q[:, cols], h_b[:, :], uv2_b[:, cols], start=False, stop=True)
                mm.then_inc(q_ps, 1)

            def main(over):
                def step(m, j):
                    now, after, before, past = (m, j), tile(m, j, 1), tile(m, j, -1), tile(m, j, -2)
                    if exists(*after):
                        neighbours(*after)
                        if over:
                            general(*after)
                    if exists(*now):
                        product(*now, 0, 12)
                    if exists(*after):
                        turn_y(*after)
                    if exists(*now):
                        product(*now, 12, 25)
                    if exists(*past):
                        ffn_out(*past)
                    if exists(*now):
                        product(*now, 25, 39)
                    if exists(*before):
                        turn_x(*before)
                    if exists(*now):
                        product(*now, 39, 48)
                    if exists(*before):
                        ffn_in(*before)

                if over:
                    pe.sem_inc(o_used, 1)
                steps(pe, step)

            pe.wait_ge(over_ready, 1)
            over = pe.value_load(over_i[0:1, 0:1], min_val=0, max_val=1)
            with pe.If(over > 0):
                main(True)
            with pe.Else():
                main(False)


_INS = ["x", "src", "dst", "L0_gnn_W", "L0_gnn_b", "L0_ffn_U1", "L0_ffn_V1", "L0_ffn_b1", "L0_ffn_U2", "L0_ffn_V2",
        "L0_ffn_b2"]


def kernel(**inputs):
    import numpy as np
    import concourse.bacc as bacc
    from concourse.bass_utils import run_bass_kernel_spmd

    nc = bacc.Bacc("TRN2", target_bir_lowering=False, num_devices=1)
    arrays, args = {}, []
    for name in _INS:
        a = np.ascontiguousarray(inputs[name])
        arrays[f"in_{name}"] = a
        args.append(nc.dram_tensor(f"in_{name}", a.shape, mybir.dt.from_np(a.dtype), kind="ExternalInput").ap())
    out = nc.dram_tensor("out", inputs["x"].shape, mybir.dt.float32, kind="ExternalOutput").ap()
    gcn_ffn(nc, *args, out)
    r = run_bass_kernel_spmd(nc, [arrays], core_ids=[0])
    return r.results[0]["out"]
```

```python
from contextlib import ExitStack

import concourse.bass as bass
from concourse import mybir



def gcn_ffn(nc, x, src, dst, W, b, U1, V1, b1, U2, V2, b2, out):
    F32, F32R, F16, I32 = mybir.dt.float32, mybir.dt.float32r, mybir.dt.float16, mybir.dt.int32
    ALU = mybir.AluOpType
    ACT = mybir.ActivationFunctionType
    AX = mybir.AxisListType

    P = 128
    N, D = x.shape
    E = src.shape[0]
    RANK, FF = V1.shape
    EPS = 1e-5
    NT = (N + P - 1) // P
    LAST = N - (NT - 1) * P
    EP = max(p for p in range(1, P + 1) if E % p == 0)
    EC = E // EP
    KC = D // P
    RC = RANK // P
    H2 = D // 2
    SLOTS = P // 2
    WB = 4
    B = 4
    YB = 2
    BIG = 1000.0
    ROOT = -256.0 / 3.0
    LINKS = 9
    CUTS = (12, 19, 36, 40)
    GROUP = 5
    RING = 4
    TURNS = EC // (RING * GROUP)
    LATE = TURNS * 7 // 10
    assert EC == TURNS * RING * GROUP and 2 <= LATE < TURNS and GROUP * NT <= H2 and N <= 7 * 2048 and D == 1024

    ctx = ExitStack()
    with ctx:
        def sb(name, shape, dt):
            return ctx.enter_context(nc.sbuf_tensor(name, shape, dt))

        def sem(name):
            return ctx.enter_context(nc.semaphore(name))

        w_hi = sb("w_hi", [P, KC, D], F32R)
        w_lo = sb("w_lo", [P, KC, D], F32R)
        yt_hi = sb("yt_hi", [P, YB, D], F32R)
        yt_lo = sb("yt_lo", [P, YB, D], F32R)
        in_tile = sb("in_tile", [P, max(NT * EC, 6 * D)], F16)
        gn_hi_t = in_tile[:, 0:2 * D].bitcast(F32R)
        in_tile3 = in_tile[:, 0:NT * EC].rearrange("p (t c) -> p t c", c=EC)

        shared = sb("shared", [P, 19 * D], F32)
        g_t = shared[:, 0:4 * D].rearrange("p (b d) -> p b d", b=B)
        x_t = shared[:, 4 * D:8 * D].rearrange("p (b d) -> p b d", b=B)
        xs_t = shared[:, 8 * D:9 * D]
        y_t = shared[:, 9 * D:10 * D]
        x1n_t = shared[:, 10 * D:11 * D]
        xt_t = shared[:, 11 * D:12 * D]
        x1_t = shared[:, 12 * D:16 * D].rearrange("p (b d) -> p b d", b=B)
        z_t = shared[:, 16 * D:17 * D]
        b_all = shared[:, 17 * D:18 * D]
        gn_t = shared[:, 18 * D:19 * D]
        og_t = in_tile[:, 2 * D:4 * D].bitcast(F32)
        on_t = in_tile[:, 4 * D:6 * D].bitcast(F32)
        not_first = shared[:, 0:4 * D].bitcast(F16)[0:EP, 0:NT * EC]
        count = shared[:, 4 * D:8 * D].bitcast(F16)[0:EP, 0:NT * EC]
        count3 = count.rearrange("p (t c) -> p t c", c=EC)
        u1T = shared[:, 8 * D:10 * D].rearrange("p (r n) -> p r n", r=RC)
        v2_t = shared[:, 10 * D:12 * D].rearrange("p (r n) -> p r n", r=RC)
        w_stage = shared[:, 12 * D:16 * D].rearrange("p (k n) -> p k n", k=WB)
        hots = shared[:, 8 * D:12 * D].bitcast(F16)
        node_hot = hots[:, 0:RING * GROUP * P].rearrange("p (b g n) -> p b g n", b=RING, g=GROUP)
        slot_hot = hots[:, 3 * D:3 * D + RING * GROUP * SLOTS].rearrange("p (b g n) -> p b g n", b=RING, g=GROUP)
        slot_val = hots[:, 5 * D:5 * D + 2 * RING * GROUP * SLOTS].rearrange("p (b g v n) -> p b g v n", b=RING, g=GROUP, v=2)
        u1_t = shared[:, 12 * D:14 * D].rearrange("p (k r) -> p k r", k=KC)
        b2_t = shared[:, 18 * D:19 * D]
        (tq, empty, deg, dinv_a, dinv_y, dinv2, loops1, nb_from, nb_lo, nb_hi, code_i) = (
            shared[:, 14 * D + i * NT:14 * D + (i + 1) * NT] for i in range(11))
        nb_from, nb_lo, nb_hi, code_i = (a.bitcast(I32) for a in (nb_from, nb_lo, nb_hi, code_i))
        SMALL = 16 * D + 14 * EC
        u2_t = shared[:, SMALL:SMALL + RANK]
        v1_t = shared[:, SMALL + RANK:SMALL + RANK + RC * FF].rearrange("p (r f) -> p r f", r=RC)
        u2T = shared[:, SMALL + 384:SMALL + 384 + RC * 2 * FF].rearrange("p (r c f) -> p r c f", r=RC, c=2)
        loop_hot = shared[:, 0:4 * D].bitcast(F16)[0:EP, 0:NT * EC].rearrange("p (g n) -> p g n", g=EC // GROUP)
        edge = [shared[:, 16 * D + i * EC:16 * D + (i + 1) * EC] for i in range(14)]
        tile_i, low_i, shi_e, dst_i, top_i, digit_i = (a.bitcast(I32) for a in edge[0:6])
        tile_f, loop_f = edge[6:8]
        tile_lp = edge[8]
        tile_nb16, low16, rank16, digit1, digit2 = (a.bitcast(F16)[:, 0:EC] for a in edge[9:14])
        assert NT * EC <= 8 * D and 14 * EC + 640 <= 2 * D and 11 * NT <= D and KC * RANK <= 2 * D and KC == 8 and RC * D <= 2 * D
        assert RC * FF <= 128 and RANK <= 256 and RING * GROUP * P <= 3 * D and SLOTS <= P // 2 and FF == 64

        gn_r = sb("gn_r", [P, D], F32R)
        uv1 = sb("uv1", [P, KC, 2, FF], F32R)
        xt_r = sb("xt_r", [P, KC, 2, P], F32R)
        uv2_a = sb("uv2_a", [P, D], F32R)
        uv2_b = sb("uv2_b", [P, D], F32R)
        b1_t = sb("b1_t", [P, 1], F32)
        h_sum = sb("h_sum", [P, P], F32)
        h_t = sb("h_t", [P, P], F32)
        h_a = sb("h_a", [P, P], F32R)
        h_b = sb("h_b", [P, P], F32R)
        ident = sb("ident", [P, P], F32)
        fold = sb("fold", [P, P], F32)
        below = sb("below", [P, P], F16)
        iota_t = sb("iota_t", [P, NT], F32)
        iota_t16 = sb("iota_t16", [P, NT], F16)
        iota_self = sb("iota_self", [P, NT], F16)
        iota_1 = sb("iota_1", [P, P], F32)
        iota_16 = sb("iota_16", [P, P], F16)
        src_i = sb("src_i", [P, EC + 1], I32)
        didx_e = sb("didx_e", [P, EC + 1], I32)
        low1 = sb("low1", [P, EC], F32)
        tile_nb = sb("tile_nb", [P, EC], F32)
        rank1 = sb("rank1", [P, EC], F32)
        nb_src = sb("nb_src", [P, NT], I32)
        nb_didx = sb("nb_didx", [P, NT], I32)
        nb_row = sb("nb_row", [P, NT], F32)
        dinv = sb("dinv", [P, NT], F32)
        own_sc = sb("own_sc", [P, NT], F32)
        own_bi = sb("own_bi", [P, NT], F32)
        base_t = sb("base_t", [P, NT], F32)
        most = sb("most", [P, 1], F32)
        most_row = sb("most_row", [1, 1], F32)
        over_i = sb("over_i", [1, 1], I32)
        ln_st = sb("ln_st", [P, 3, 2, 6], F32)
        ln_mv = sb("ln_mv", [P, 3, 2], F32)
        ln_v = sb("ln_v", [P, 3], F32)
        ln_a = sb("ln_a", [P, 3], F32)
        ln_y = sb("ln_y", [P, 3], F32)
        x_sc = sb("x_sc", [P, B, 1], F32)
        x_bi = sb("x_bi", [P, B, 1], F32)
        g_sc = sb("g_sc", [P, B, 1], F32)
        f_sc = sb("f_sc", [P, B, 1], F32)
        f_bi = sb("f_bi", [P, B, 1], F32)
        idx_src = sb("idx_src", [P, B], I32)
        idx_dinv = sb("idx_dinv", [P, B], I32)
        g_dinv = sb("g_dinv", [P, B], F32)
        spread = sb("spread", [P, B, P], F32R)
        o_src = sb("o_src", [P, 2], I32)
        o_didx = sb("o_didx", [P, 2], I32)
        o_dinv = sb("o_dinv", [P, 1], F32)
        o_st = sb("o_st", [P, 2, 6], F32)
        o_mv = sb("o_mv", [P, 2], F32)
        o_v = sb("o_v", [P, 1], F32)
        o_a = sb("o_a", [P, 1], F32)
        o_y = sb("o_y", [P, 1], F32)
        o_sc = sb("o_sc", [P, 1], F32)
        o_late = sb("o_late", [P, 1], F32)
        o_mine = sb("o_mine", [P, 1], F32)
        o_hot = sb("o_hot", [P, P], F32)

        ps_a = ctx.enter_context(nc.psum_tensor("ps_a", [P, D], F32))
        ps_z = ctx.enter_context(nc.psum_tensor("ps_z", [P, D], F32))
        ps_t = ctx.enter_context(nc.psum_tensor("ps_t", [P, D], F32))
        ps_q = ctx.enter_context(nc.psum_tensor("ps_q", [P, D], F32))
        dinv_dram = nc.dram_tensor("dinv_dram", [P * NT, 1], F32, kind="Internal").ap()

        src_in, dst_in, u_in, b1_in, b_all_in = (sem(n) for n in ("src_in", "dst_in", "u_in", "b1_in", "b_all_in"))
        w_in = [sem(f"w_in{k}") for k in range(KC)]
        consts = sem("consts")
        prep = sem("prep")
        tiles_ready = sem("tiles_ready")
        mask_ready = sem("mask_ready")
        ident_ready = sem("ident_ready")
        u1T_ps, u1T_sb, u2T_ps, u2T_sb = sem("u1T_ps"), sem("u1T_sb"), sem("u2T_ps"), sem("u2T_sb")
        uv1_ps, uv2_ps, uv_ready = sem("uv1_ps"), sem("uv2_ps"), sem("uv_ready")
        w_hi_ready, w_lo_ready = sem("w_hi_ready"), sem("w_lo_ready")
        count_in, base_ready = sem("count_in"), sem("base_ready")
        scanned, digits_ready = sem("scanned"), sem("digits_ready")
        b2_in, uv_part = sem("b2_in"), sem("uv_part")
        slot_val_ready, loop_dist, loop_ready = sem("slot_val_ready"), sem("loop_dist"), sem("loop_ready")
        tq_ready, digits_ps = sem("tq_ready"), sem("digits_ps")
        hot_ready, hot_used = sem("hot_ready"), sem("hot_used")
        slot_ready, slot_used = sem("slot_ready"), sem("slot_used")
        most_ready, most_ps = sem("most_ready"), sem("most_ps")
        over_ready = sem("over_ready")
        tables_ready, dinv_ready = sem("tables_ready"), sem("dinv_ready")
        dinv_out = sem("dinv_out")
        fold_ready = sem("fold_ready")
        xT_lo, h_parts, h_summed, h_folded = sem("xT_lo"), sem("h_parts"), sem("h_summed"), sem("h_folded")
        g_zero, g_rest_zero = sem("g_zero"), sem("g_rest_zero")
        h_one = sem("h_one")
        gn_hi, gn_lo, h_gelu, h_hi = sem("gn_hi"), sem("gn_lo"), sem("h_gelu"), sem("h_hi")
        x_in = [sem(f"x_in{j}") for j in range(B)]
        g_in = [sem(f"g_in{j}") for j in range(B)]
        d_in = [sem(f"d_in{j}") for j in range(B)]
        out_done = [sem(f"out_done{j}") for j in range(B)]
        idx_ready = sem("idx_ready")
        coef_link = sem("coef_link")
        x_coef, g_coef, f_coef = sem("x_coef"), sem("g_coef"), sem("f_coef")
        spread_ready, gn_ready, xs_ready = sem("spread_ready"), sem("gn_ready"), sem("xs_ready")
        nb_sum, y_ready, yT_ps, yT_hi, yT_lo = (sem(n) for n in ("nb_sum", "y_ready", "yT_ps", "yT_hi", "yT_lo"))
        z_ps, z_biased, z_relu, x1_ready, x1n_ready = (sem(n) for n in ("z_ps", "z_biased", "z_relu", "x1_ready", "x1n_ready"))
        xT_ps, xT_ready, h_ps, h_ready, q_ps, out_ready = (sem(n) for n in ("xT_ps", "xT_ready", "h_ps", "h_ready", "q_ps", "out_ready"))
        o_idx, o_in, o_din, o_chain, o_ready, o_used = (sem(n) for n in ("o_idx", "o_in", "o_din", "o_chain", "o_ready", "o_used"))

        block = ctx.enter_context(nc.Block())

        def tile(m, j, shift):
            j += shift
            return m + j // B, j % B

        def number(m, j):
            return m * B + j

        def steps(eng, step):
            first, last = 2, (NT - 5) // B
            for i in range(-2, B * first):
                step(i // B, i % B)
            with eng.Fori(first, last) as m:
                for j in range(B):
                    step(m, j)
            for i in range(B * last, NT + 2):
                step(i // B, i % B)

        def exists(m, j):
            return not isinstance(m, int) or 0 <= number(m, j) < NT

        def wait(eng, s, value):
            if not isinstance(value, int) or value > 0:
                eng.wait_ge(s, value)

        @block.sync
        def _(sp):
            sp.dma_start(dst_i[0:EP, :], dst.rearrange("(p c) -> p c", p=EP)).then_inc(dst_in, 16)
            sp.dma_start(src_i[0:EP, 0:EC], src.rearrange("(p c) -> p c", p=EP)).then_inc(src_in, 16)
            sp.dma_start(u1_t, U1.rearrange("(k p) r -> p k r", p=P)).then_inc(u_in, 16)
            sp.dma_start(u2_t[0:FF, :], U2).then_inc(u_in, 16)
            sp.dma_start(v1_t, V1.rearrange("(r p) f -> p r f", p=P)).then_inc(u_in, 16)
            sp.dma_start(v2_t, V2.rearrange("(r p) n -> p r n", p=P)).then_inc(u_in, 16)
            for half in range(2):
                sp.dma_start(b1_t[half * FF:(half + 1) * FF, :], b1.rearrange("(f o) -> f o", o=1)).then_inc(b1_in, 16)
            for row in (64, 96):
                sp.dma_start(b2_t[row:row + 1, :], b2.rearrange("(o n) -> o n", o=1)).then_inc(b2_in, 16)
            for k in range(KC):
                if k == 2:
                    sp.wait_ge(u1T_ps, 1)
                if k >= WB:
                    sp.wait_ge(w_lo_ready, k - WB + 1)
                sp.dma_start(w_stage[:, (k + 2) % WB, :], W[k * P:(k + 1) * P, :]).then_inc(w_in[k], 16)

            def load(m, j):
                rows = LAST if isinstance(m, int) and number(m, j) == NT - 1 else P
                wait(sp, x1_ready, number(m, j) - B + 1)
                sp.dma_start(x_t[0:rows, j, :], x[bass.ds(number(m, j) * P, rows), :]).then_inc(x_in[j], 16)

            sp.wait_ge(most_ready, 1)
            for t in range(B):
                load(0, t)
            sp.wait_ge(hot_used, EC // GROUP)
            sp.wait_ge(slot_used, EC // GROUP)
            sp.wait_ge(dinv_ready, 1)
            sp.dma_start(dinv_dram.rearrange("(p t) o -> p (t o)", p=P), dinv[:, :]).then_inc(dinv_out, 16)
            sp.dma_start(b_all, b.rearrange("(o n) -> o n", o=1).broadcast_to([P, D])).then_inc(b_all_in, 16)

            def store(m, j):
                rows = LAST if isinstance(m, int) and number(m, j) == NT - 1 else P
                sp.wait_ge(out_ready, number(m, j) + 1)
                sp.dma_start(out[bass.ds(number(m, j) * P, rows), :], x1_t[0:rows, j, :]).then_inc(out_done[j], 16)

            def step(m, j):
                for shift, what in ((3, load), (-2, store)):
                    tm, tj = tile(m, j, shift)
                    if exists(tm, tj) and not (what is load and isinstance(tm, int) and number(tm, tj) < B):
                        what(tm, tj)

            steps(sp, step)
            for j in range(B):
                sp.wait_ge(out_done[j], 16 * len(range(j, NT, B)))
            sp.wait_ge(dinv_out, 16)

        @block.gpsimd
        def _(pool):
            pool.memset(ident[:, :], 0.0).then_inc(ident_ready, 1)
            pool.memset(below[:, :], 0.0).then_inc(ident_ready, 1)
            pool.wait_ge(ident_ready, 2)
            pool.affine_select(out=ident[:, :], in_=ident[:, :], compare_op=ALU.not_equal, fill=1.0, base=0,
                               pattern=[[-1, P]], channel_multiplier=1).then_inc(ident_ready, 1)
            pool.affine_select(out=below[:, :], in_=below[:, :], compare_op=ALU.is_ge, fill=1.0, base=0,
                               pattern=[[-1, P]], channel_multiplier=1).then_inc(ident_ready, 1)
            pool.memset(fold[:, :], 0.0).then_inc(fold_ready, 1)
            for i, base in enumerate((0, FF, -FF)):
                pool.wait_ge(fold_ready, i + 1)
                pool.affine_select(out=fold[:, :], in_=fold[:, :], compare_op=ALU.not_equal, fill=1.0, base=base,
                                   pattern=[[-1, P]], channel_multiplier=1).then_inc(fold_ready, 1)
            for table, base in ((iota_t, 0), (iota_t16, 0), (iota_self, int(BIG)), (iota_1, 1), (iota_16, 1)):
                pool.iota(table[:, :], [[1, table.shape[1]]], base=base, channel_multiplier=0,
                          allow_small_or_imprecise_dtypes=True).then_inc(consts, 1)
            pool.memset(not_first, 1.0).then_inc(mask_ready, 1)
            pool.wait_ge(mask_ready, 1)
            pool.memset(not_first.rearrange("p (t c) -> p t c", c=EC)[:, :, 0:1], 0.0).then_inc(mask_ready, 1)
            pool.memset(h_b[:, :].bitcast(F32), 1.0).then_inc(h_one, 1)
            pool.memset(uv2_b[:, :].bitcast(F32), 0.0).then_inc(h_one, 1)
            for k in range(KC):
                pool.wait_ge(w_hi_ready, k + 1)
                pool.tensor_tensor(w_lo[:, k, :], w_stage[:, (k + 2) % WB, :], w_hi[:, k, :].bitcast(F32),
                                   ALU.subtract).then_inc(w_lo_ready, 1)

            def slot_values(q):
                for r in range(RING):
                    g = q * RING + r
                    wait(pool, slot_used, g - RING + 1)
                    pool.wait_ge(slot_ready, g + 1)
                    for v, digit in enumerate((digit1, digit2)):
                        pool.tensor_tensor(slot_val[0:EP, r, :, v, :], slot_hot[0:EP, r],
                                           digit[0:EP, bass.ds(g * GROUP, GROUP), None].to_broadcast([EP, GROUP, SLOTS]),
                                           ALU.mult).then_inc(slot_val_ready, 1)

            slot_values(0)
            with pool.Fori(1, TURNS) as q:
                slot_values(q)
            pool.memset(g_dinv[:, :], 0.0).then_inc(g_zero, 1)
            pool.wait_ge(hot_used, EC // GROUP)
            pool.memset(g_t[:, 0, :], 0.0).then_inc(g_zero, 1)
            pool.wait_ge(slot_used, EC // GROUP)
            pool.memset(in_tile[:, 0:2 * D].bitcast(F32), 0.0).then_inc(g_zero, 1)
            pool.wait_ge(tables_ready, 1)

            last_row = pool.to_reg(N - 1)
            last_dinv = pool.to_reg(P * NT - 1)

            def stage(m, j):
                t = number(m, j)
                wait(pool, g_in[j], m * 16)
                wait(pool, d_in[j], m * 16)
                pool.tensor_copy(idx_src[:, j:j + 1], nb_src[:, bass.ds(t, 1)]).then_inc(idx_ready, 1)
                pool.tensor_copy(idx_dinv[:, j:j + 1], nb_didx[:, bass.ds(t, 1)]).then_inc(idx_ready, 1)

            def gather_rows(m, j):
                t = number(m, j)
                pool.wait_ge(idx_ready, t * 2 + 2)
                wait(pool, gn_ready, t - B + 1)
                if exists(*tile(m, j, 1)):
                    stage(*tile(m, j, 1))
                pool.indirect_dma_start(
                    out=g_t[:, j, :], out_offset=None, in_=x,
                    in_offset=bass.IndirectOffsetOnAxis(ap=idx_src[:, j:j + 1], axis=0),
                    bounds_check=last_row, oob_is_err=False).then_inc(g_in[j], 16)

            def gather_dinv(m, j):
                pool.indirect_dma_start(
                    out=g_dinv[:, j:j + 1], out_offset=None, in_=dinv_dram,
                    in_offset=bass.IndirectOffsetOnAxis(ap=idx_dinv[:, j:j + 1], axis=0),
                    bounds_check=last_dinv, oob_is_err=False).then_inc(d_in[j], 16)

            def low_rows(m, j):
                t = number(m, j)
                pool.wait_ge(gn_ready, t + 1)
                pool.wait_ge(gn_hi, t + 1)
                wait(pool, nb_sum, t)
                pool.tensor_tensor(gn_r[:, :], gn_t, gn_hi_t.bitcast(F32),
                                   ALU.subtract).then_inc(gn_lo, 1)

            def low_transposed(m, j):
                t = number(m, j)
                pool.wait_ge(xT_ready, t + 1)
                pool.tensor_tensor(xt_r[:, :, 1, :], xt_t.rearrange("p (k n) -> p k n", k=KC),
                                   xt_r[:, :, 0, :].bitcast(F32), ALU.subtract).then_inc(xT_lo, 1)

            def residual(m, j):
                t = number(m, j)
                pool.wait_ge(z_relu, t + 1)
                wait(pool, out_done[j], m * 16)
                pool.tensor_tensor(x1_t[:, j, :], z_t, x_t[:, j, :], ALU.add).then_inc(x1_ready, 1)

            def general(m, j):
                t = number(m, j)
                with pool.Fori(0, EC // 2) as q:
                    for r in range(2):
                        n = t * EC + q * 2 + r
                        pool.wait_ge(o_idx, n * 2 + 2)
                        pool.wait_ge(o_ready, n + 1)
                        stage_edges(q * 2 + r + 1, 1 - r)
                        pool.indirect_dma_start(
                            out=og_t[0:EP, :], out_offset=None, in_=x,
                            in_offset=bass.IndirectOffsetOnAxis(ap=o_src[0:EP, r:r + 1], axis=0),
                            bounds_check=last_row, oob_is_err=False).then_inc(o_in, 16)
                        pool.indirect_dma_start(
                            out=o_dinv[0:EP, :], out_offset=None, in_=dinv_dram,
                            in_offset=bass.IndirectOffsetOnAxis(ap=o_didx[0:EP, r:r + 1], axis=0),
                            bounds_check=last_dinv, oob_is_err=False).then_inc(o_din, 16)

            def stage_edges(c, r):
                pool.tensor_copy(o_src[0:EP, r:r + 1], src_i[0:EP, bass.ds(c, 1)]).then_inc(o_idx, 1)
                pool.tensor_copy(o_didx[0:EP, r:r + 1], didx_e[0:EP, bass.ds(c, 1)]).then_inc(o_idx, 1)

            def main(over):
                if over:
                    stage_edges(0, 0)

                def step(m, j):
                    tm, tj = tile(m, j, -1)
                    if exists(tm, tj):
                        residual(tm, tj)
                    tm, tj = tile(m, j, 1)
                    if over and exists(tm, tj):
                        general(tm, tj)
                    tm, tj = tile(m, j, 4)
                    if exists(tm, tj):
                        gather_rows(tm, tj)
                        gather_dinv(tm, tj)
                    tm, tj = tile(m, j, 2)
                    if exists(tm, tj):
                        low_rows(tm, tj)
                    tm, tj = tile(m, j, -1)
                    if exists(tm, tj):
                        low_transposed(tm, tj)

                steps(pool, step)

            stage(0, 0)
            pool.wait_ge(g_zero, 3)
            gather_rows(0, 0)
            pool.wait_ge(g_rest_zero, 1)
            gather_rows(0, 1)
            pool.wait_ge(dinv_out, 16)
            for t in range(2):
                gather_dinv(0, t)
            pool.wait_ge(over_ready, 1)
            over = pool.value_load(over_i[0:1, 0:1], min_val=0, max_val=1)
            with pool.If(over > 0):
                main(True)
            with pool.Else():
                main(False)

        @block.scalar
        def _(act):
            def split_w(k):
                act.wait_ge(w_in[k], 16)
                act.copy(w_hi[:, k, :], w_stage[:, (k + 2) % WB, :]).then_inc(w_hi_ready, 1)

            for k in range(2):
                split_w(k)
            act.wait_ge(u1T_ps, 1)
            act.copy(u1T[:, 0, :], ps_t[:, :]).then_inc(u1T_sb, 1)
            act.copy(u1T[:, 1, :], ps_q[:, :]).then_inc(u1T_sb, 1)
            act.wait_ge(u2T_ps, 1)
            for c in range(2):
                act.copy(u2T[:, :, c, :], ps_z[:, 0:RC * FF].rearrange("p (r f) -> p r f", r=RC)).then_inc(u2T_sb, 1)
            for k in range(2, 4):
                split_w(k)
            act.wait_ge(uv1_ps, 1)
            act.copy(uv1[:, :, 0, :], ps_t[:, 0:KC * FF].rearrange("p (k f) -> p k f", k=KC)).then_inc(uv_ready, 1)
            act.wait_ge(uv2_ps, 1)
            act.copy(uv2_a[:, :], ps_q[:, :]).then_inc(uv_ready, 1)
            act.wait_ge(b2_in, 32)
            act.wait_ge(h_one, 2)
            for row in (64, 96):
                act.copy(uv2_b[row:row + 1, :], b2_t[row:row + 1, :]).then_inc(uv_ready, 1)
            for k in range(4, KC):
                split_w(k)
            act.wait_ge(consts, 5)
            act.wait_ge(digits_ready, 2)
            act.wait_ge(scanned, 1)
            parts = 4
            for part in range(parts):
                first, end = RING * LATE * part // parts, RING * LATE * (part + 1) // parts
                with act.Fori(first, end) as g:
                    for k in range(GROUP):
                        dist = act.activation(loop_hot[:, bass.ds(g, 1), k * NT:(k + 1) * NT], iota_self[0:EP, None, :],
                                              ACT.Abs, bias=tile_lp[0:EP, bass.ds(g * GROUP + k, 1)], scale=-1.0)
                    dist.then_inc(loop_dist, 1)
                act.wait_ge(loop_dist, end)
                with act.Fori(first, end) as g:
                    act.activation(loop_hot[:, bass.ds(g, 1), :], loop_hot[:, bass.ds(g, 1), :], ACT.Relu,
                                   bias=iota_1[0:EP, 0:1], scale=-1.0).then_inc(loop_ready, 1)

            act.wait_ge(hot_used, EC // GROUP)
            act.wait_ge(g_zero, 1)
            act.copy(shared[:, D:B * D], g_dinv[:, 0:1].to_broadcast([P, (B - 1) * D])).then_inc(g_rest_zero, 1)

            def high_rows(m, j):
                t = number(m, j)
                act.wait_ge(gn_ready, t + 1)
                wait(act, gn_lo, t)
                act.copy(gn_hi_t[SLOTS:P, :], gn_t[SLOTS:P, :]).then_inc(gn_hi, 1)

            def own_rows(m, j):
                t = number(m, j)
                act.wait_ge(x_coef, t + 1)
                wait(act, y_ready, t)
                act.activation(xs_t, x_t[:, j, :], ACT.Identity, bias=x_bi[:, j, :],
                               scale=x_sc[:, j, :]).then_inc(xs_ready, 1)

            def high_part(m, j):
                t = number(m, j)
                act.wait_ge(yT_ps, t + 1)
                wait(act, z_ps, (t - YB + 1) * 2)
                act.copy(yt_hi[:, j % YB, :], ps_t[:, :]).then_inc(yT_hi, 1)

            def relu(m, j):
                t = number(m, j)
                act.wait_ge(z_biased, t * 2 + 2)
                act.activation(z_t, z_t, ACT.Relu).then_inc(z_relu, 1)

            def normalise(m, j):
                t = number(m, j)
                act.wait_ge(f_coef, t + 1)
                wait(act, xT_ps, t)
                act.activation(x1n_t, x1_t[:, j, :], ACT.Identity, bias=f_bi[:, j, :],
                               scale=f_sc[:, j, :]).then_inc(x1n_ready, 1)

            def transposed(m, j):
                t = number(m, j)
                act.wait_ge(xT_ps, t + 1)
                wait(act, h_ps, t)
                act.copy(xt_r[:, :, 0, :], ps_t[:, :].rearrange("p (k n) -> p k n", k=KC))
                act.copy(xt_t, ps_t[:, :]).then_inc(xT_ready, 1)

            def hidden_parts(m, j):
                t = number(m, j)
                act.wait_ge(h_ps, t + 1)
                wait(act, h_folded, t)
                act.copy(h_sum[:, :], ps_q[:, 0:P]).then_inc(h_parts, 1)

            def hidden(m, j):
                t = number(m, j)
                act.wait_ge(h_folded, t + 1)
                wait(act, h_ready, t * 2)
                act.activation(h_t[:, :], ps_q[:, H2:H2 + P], ACT.Gelu_apprx_tanh, bias=b1_t[:, :],
                               scale=1.0).then_inc(h_gelu, 1)

            def hidden_high(m, j):
                t = number(m, j)
                act.wait_ge(h_gelu, t + 1)
                wait(act, q_ps, t)
                act.copy(h_a[:, :], h_t[:, :]).then_inc(h_hi, 1)
                act.copy(h_b[0:FF, :], h_t[0:FF, :]).then_inc(h_ready, 1)

            def step(m, j):
                order = [(-2, hidden_parts), (1, high_part), (-2, hidden), (-2, hidden_high), (-1, normalise), (2, high_rows),
                         (2, own_rows), (-1, transposed), (0, relu)]
                if isinstance(m, int) and number(m, j) == -1:
                    order = [(2, high_rows), (1, high_part), (2, own_rows)]
                for shift, what in order:
                    tm, tj = tile(m, j, shift)
                    if exists(tm, tj):
                        what(tm, tj)

            act.wait_ge(b1_in, 32)
            act.wait_ge(g_zero, 3)
            steps(act, step)

        @block.vector
        def _(dve):
            n = 0

            def chain(ins):
                nonlocal n
                n += 1
                ins.then_inc(prep, 1)
                dve.wait_ge(prep, n)

            def inverse_root(v, a, y, link):
                def square():
                    if len(v.shape) == 2 and v.shape[1] <= 3:
                        for c in range(v.shape[1]):
                            ins = dve.scalar_tensor_tensor(a[:, c:c + 1], y[:, c:c + 1], y[:, c:c + 1], v[:, c:c + 1],
                                                           ALU.mult, ALU.mult)
                        link(ins)
                    else:
                        link(dve.tensor_tensor(a, y, y, ALU.mult))
                        link(dve.tensor_tensor(a, a, v, ALU.mult))

                link(dve.tensor_scalar(y.bitcast(I32), v.bitcast(I32), -0.5, float(0x5F3759DF), ALU.mult, ALU.add))
                square()
                link(dve.scalar_tensor_tensor(y, a, 3.0, y, ALU.subtract, ALU.mult))
                square()
                link(dve.scalar_tensor_tensor(a, a, 40.0 / 3.0, a, ALU.subtract, ALU.mult))
                link(dve.scalar_tensor_tensor(y, a, 80.0, y, ALU.add, ALU.mult))

            e = slice(0, EP)
            dve.wait_ge(dst_in, 16)
            dve.wait_ge(src_in, 16)
            dve.tensor_scalar(tile_i[e, :], dst_i[e, :], 7, None, ALU.arith_shift_right)
            dve.tensor_scalar(low_i[e, :], dst_i[e, :], P - 1, None, ALU.bitwise_and)
            dve.tensor_scalar(shi_e[e, :], src_i[e, 0:EC], 7, None, ALU.arith_shift_right)
            dve.tensor_scalar(didx_e[e, 0:EC], src_i[e, 0:EC], P - 1, None, ALU.bitwise_and)
            dve.tensor_scalar(top_i[e, :], src_i[e, 0:EC], 11, None, ALU.arith_shift_right)
            dve.tensor_scalar(digit_i[e, :], src_i[e, 0:EC], 2047, None, ALU.bitwise_and)
            chain(dve.tensor_tensor(loop_f[e, :], src_i[e, 0:EC], dst_i[e, :], ALU.is_equal))
            dve.tensor_scalar(tile_f[e, :], tile_i[e, :], 0.0, None, ALU.add)
            chain(dve.tensor_scalar(low1[e, :], low_i[e, :], 1.0, None, ALU.add))
            dve.scalar_tensor_tensor(didx_e[e, 0:EC], didx_e[e, 0:EC], float(NT), shi_e[e, :], ALU.mult, ALU.add)
            dve.tensor_copy(src_i[e, EC:EC + 1], src_i[e, 0:1])
            dve.tensor_scalar(digit1[e, :], digit_i[e, :], 0.0, None, ALU.add)
            dve.scalar_tensor_tensor(digit2[e, :], top_i[e, :], 256.0, low1[e, :], ALU.mult,
                                     ALU.add).then_inc(digits_ready, 1)
            dve.scalar_tensor_tensor(tile_nb16[e, :], loop_f[e, :], -BIG, tile_f[e, :], ALU.mult, ALU.add)
            chain(dve.scalar_tensor_tensor(tile_nb[e, :], loop_f[e, :], -BIG, tile_f[e, :], ALU.mult, ALU.add))
            dve.wait_ge(consts, 5)
            dve.tensor_tensor(in_tile3[e], iota_t16[e, :, None].to_broadcast([EP, NT, EC]),
                              tile_nb16[e, None, :].to_broadcast([EP, NT, EC]), ALU.is_equal).then_inc(tiles_ready, 1)
            dve.scalar_tensor_tensor(tile_lp[e, :], loop_f[e, :], BIG, tile_f[e, :], ALU.mult, ALU.add)
            dve.tensor_copy(low16[e, :], low1[e, :]).then_inc(digits_ready, 1)
            dve.tensor_copy(didx_e[e, EC:EC + 1], didx_e[e, 0:1])
            dve.wait_ge(tiles_ready, 1)
            dve.tensor_copy(count, in_tile[e, 0:NT * EC]).then_inc(count_in, 1)
            dve.wait_ge(base_ready, 1)
            chain(dve.tensor_reduce(base_t[:, :], ps_a[:, 0:NT * GROUP].rearrange("p (t g) -> p t g", g=GROUP), AX.X, ALU.add))
            dve.tensor_scalar(base_t[:, :], base_t[:, :], 1024.0, None, ALU.min).then_inc(count_in, 1)
            dve.wait_ge(count_in, 2)
            chain(dve.tensor_tensor(count3[:, :, 0:1], count3[:, :, 0:1], base_t[e, :, None], ALU.add))
            dve.wait_ge(mask_ready, 2)
            dve.tensor_tensor_scan(count, not_first, count, 0.0, ALU.mult, ALU.add).then_inc(scanned, 1)
            dve.wait_ge(scanned, 1)
            chain(dve.tensor_tensor(count, count, in_tile[e, 0:NT * EC], ALU.mult))
            left = NT
            while left > 1:
                low, left = left // 2, (left + 1) // 2
                chain(dve.tensor_tensor(count[:, 0:low * EC], count[:, 0:low * EC],
                                        count[:, left * EC:(left + low) * EC], ALU.add))
            dve.memset(most[:, :], 0.0)
            dve.tensor_copy(rank16[e, :], count[:, 0:EC])
            chain(dve.tensor_copy(rank1[e, :], count[:, 0:EC]))
            dve.tensor_reduce(most[e, :], rank1[e, :], AX.X, ALU.max).then_inc(most_ready, 1)
            dve.wait_ge(uv2_ps, 1)

            def slot_rows(g, r):
                wait(dve, slot_val_ready, (g - RING + 1) * 2)
                dve.tensor_tensor(slot_hot[e, r], iota_16[e, None, 0:SLOTS].to_broadcast([EP, GROUP, SLOTS]),
                                  rank16[e, bass.ds(g * GROUP, GROUP), None].to_broadcast([EP, GROUP, SLOTS]),
                                  ALU.is_equal).then_inc(slot_ready, 1)

            def hot_rows(g, r, late):
                wait(dve, hot_used, g - RING + 1)
                if late:
                    dve.tensor_tensor(loop_hot[:, bass.ds(g, 1), :].rearrange("p o (c n) -> p (o c) n", c=GROUP),
                                      iota_self[e, None, :].to_broadcast([EP, GROUP, NT]),
                                      tile_lp[e, bass.ds(g * GROUP, GROUP), None].to_broadcast([EP, GROUP, NT]),
                                      ALU.is_equal)
                dve.tensor_tensor(node_hot[e, r], iota_16[e, None, :].to_broadcast([EP, GROUP, P]),
                                  low16[e, bass.ds(g * GROUP, GROUP), None].to_broadcast([EP, GROUP, P]),
                                  ALU.is_equal).then_inc(hot_ready, 1)

            def one_hots(q, late):
                for r in range(RING):
                    slot_rows(q * RING + r, r)
                    hot_rows(q * RING + r, r, late)

            one_hots(0, False)
            for start, end in ((1, LATE), (LATE, TURNS)):
                with dve.Fori(start, end) as q:
                    one_hots(q, start == LATE)
            dve.wait_ge(uv_ready, 4)
            dve.wait_ge(w_lo_ready, KC)
            dve.tensor_tensor(uv1[:, :, 1, :], ps_t[:, 0:KC * FF].rearrange("p (k f) -> p k f", k=KC),
                              uv1[:, :, 0, :].bitcast(F32), ALU.subtract).then_inc(uv_part, 1)
            dve.wait_ge(hot_used, EC // GROUP)
            dve.wait_ge(slot_used, EC // GROUP)
            dve.tensor_copy(tq[:, :], ps_a[:, H2:H2 + NT]).then_inc(tq_ready, 1)
            chain(dve.tensor_scalar(loops1[:, :], ps_z[:, H2:H2 + NT], 1.0, None, ALU.add))
            chain(dve.tensor_tensor(deg[:, :], loops1[:, :], ps_z[:, 0:NT], ALU.add))
            dve.wait_ge(digits_ps, 1)
            first, second = ps_t[:, 0:NT], ps_t[:, H2:H2 + NT]
            dve.tensor_scalar(empty[:, :], second, 0.0, float(1 << 20), ALU.is_equal, ALU.mult)
            chain(dve.tensor_scalar(code_i[:, :], second, 0.0, None, ALU.add))
            dve.tensor_scalar(nb_hi[:, :], code_i[:, :], 8, None, ALU.arith_shift_right)
            chain(dve.tensor_scalar(nb_lo[:, :], code_i[:, :], 255, None, ALU.bitwise_and))
            dve.tensor_scalar(nb_row[:, :], nb_lo[:, :], 0.0, None, ALU.add)
            chain(dve.scalar_tensor_tensor(nb_from[:, :], nb_hi[:, :], 2048.0, first, ALU.mult, ALU.add))
            dve.tensor_tensor(nb_src[:, :], nb_from[:, :], empty[:, :], ALU.add)
            dve.tensor_scalar(nb_hi[:, :], nb_from[:, :], 7, None, ALU.arith_shift_right)
            chain(dve.tensor_scalar(nb_lo[:, :], nb_from[:, :], P - 1, None, ALU.bitwise_and))
            dve.scalar_tensor_tensor(nb_didx[:, :], nb_lo[:, :], float(NT), nb_hi[:, :], ALU.mult,
                                     ALU.add).then_inc(tables_ready, 1)
            dve.wait_ge(most_ps, 1)
            chain(dve.tensor_reduce(most_row[:, :], ps_t[0:1, 2 * P:3 * P], AX.X, ALU.max))
            dve.tensor_scalar(over_i[:, :], most_row[:, :], float(SLOTS), None, ALU.is_gt).then_inc(over_ready, 1)
            inverse_root(deg[:, :], dinv_a[:, :], dinv_y[:, :], chain)
            dve.tensor_scalar(dinv[:, :], dinv_y[:, :], 1.0 / ROOT, None, ALU.mult).then_inc(dinv_ready, 1)
            dve.wait_ge(dinv_ready, 1)
            chain(dve.tensor_tensor(dinv2[:, :], dinv[:, :], dinv[:, :], ALU.mult))
            dve.scalar_tensor_tensor(own_sc[:, :], dinv2[:, :], 1.0 / ROOT, loops1[:, :], ALU.mult, ALU.mult)
            chain(dve.scalar_tensor_tensor(own_bi[:, :], dinv2[:, :], -1.0 / ROOT, loops1[:, :], ALU.mult,
                                           ALU.mult))
            dve.tensor_tensor(uv2_b[96:97, :], b2_t[96:97, :], uv2_b[96:97, :].bitcast(F32),
                              ALU.subtract).then_inc(uv_part, 1)

            def links(s, start):
                done = [0]

                def link(ins):
                    done[0] += 1
                    ins.then_inc(s, 1)
                    dve.wait_ge(s, start + done[0])
                return link

            def coefs(m, j):
                ft, fj = tile(m, j, -1)
                am, aj = tile(m, j, 2)
                ffn, ahead = exists(ft, fj), exists(am, aj)
                ft, t = number(ft, fj), number(am, aj)
                link = links(coef_link, (number(m, j) + 2) * LINKS)
                which = range(0 if ffn else 1, 3 if ahead else 1)
                cols = slice(which[0], which[-1] + 1)
                if ahead:
                    dve.wait_ge(x_in[aj], am * 16 + 16)
                    for h in range(2):
                        dve.bn_stats(ln_st[:, 1, h, :], x_t[:, aj, h * H2:(h + 1) * H2])
                    dve.wait_ge(g_in[aj], am * 16 + 16)
                    for h in range(2):
                        ins = dve.bn_stats(ln_st[:, 2, h, :], g_t[:, aj, h * H2:(h + 1) * H2])
                if exists(*tile(m, j, -2)):
                    hidden_sum(*tile(m, j, -2))
                if ffn:
                    dve.wait_ge(x1_ready, ft + 1)
                    for h in range(2):
                        ins = dve.bn_stats(ln_st[:, 0, h, :], x1_t[:, fj, h * H2:(h + 1) * H2])
                if ahead:
                    wait(dve, nb_sum, t - B + 1)
                link(ins)
                if ahead:
                    dve.tensor_scalar(spread[:, aj, :], iota_1[:, :], nb_row[:, bass.ds(t, 1)], None,
                                      ALU.is_equal).then_inc(spread_ready, 1)
                for c in which:
                    ins = dve.bn_aggr(ln_mv[:, c, :], ln_st[:, c, :, :])
                link(ins)
                link(dve.tensor_scalar(ln_v[:, cols], ln_mv[:, cols, 1], EPS, None, ALU.add))
                inverse_root(ln_v[:, cols], ln_a[:, cols], ln_y[:, cols], link)
                if ffn:
                    dve.tensor_scalar(f_sc[:, fj, :], ln_y[:, 0:1], 1.0 / ROOT, None, ALU.mult)
                    dve.scalar_tensor_tensor(f_bi[:, fj, :], ln_mv[:, 0, 0:1], -1.0 / ROOT, ln_y[:, 0:1], ALU.mult,
                                             ALU.mult).then_inc(f_coef, 1)
                if ahead:
                    dve.wait_ge(d_in[aj], am * 16 + 16)
                    dve.tensor_scalar(g_sc[:, aj, :], ln_y[:, 2:3], 1.0 / ROOT, g_dinv[:, aj:aj + 1], ALU.mult,
                                      ALU.mult).then_inc(g_coef, 1)
                    dve.tensor_scalar(x_sc[:, aj, :], ln_y[:, 1:2], own_sc[:, bass.ds(t, 1)], None, ALU.mult)
                    dve.scalar_tensor_tensor(x_bi[:, aj, :], ln_mv[:, 1, 0:1], own_bi[:, bass.ds(t, 1)], ln_y[:, 1:2],
                                             ALU.mult, ALU.mult).then_inc(x_coef, 1)

            def neighbour_rows(m, j):
                t = number(m, j)
                dve.wait_ge(g_coef, t + 1)
                wait(dve, gn_lo, t)
                dve.tensor_scalar(gn_t, g_t[:, j, :], ln_mv[:, 2, 0:1], g_sc[:, j, :], ALU.subtract,
                                  ALU.mult).then_inc(gn_ready, 1)

            def hidden_sum(m, j):
                t = number(m, j)
                dve.wait_ge(h_parts, t + 1)
                dve.tensor_tensor(h_sum[:, :], ps_q[:, P:2 * P], h_sum[:, :], ALU.add).then_inc(h_summed, 1)

            def hidden_low(m, j):
                t = number(m, j)
                dve.wait_ge(h_hi, t + 1)
                dve.tensor_tensor(h_a[FF:P, :], h_t[FF:P, :], h_a[FF:P, :].bitcast(F32),
                                  ALU.subtract).then_inc(h_ready, 1)

            def add_bias(m, j):
                t = number(m, j)
                if isinstance(m, int) and t == 0:
                    dve.wait_ge(b_all_in, 16)
                wait(dve, x1_ready, t)
                for h in range(2):
                    cols = slice(h * H2, (h + 1) * H2)
                    dve.wait_ge(z_ps, t * 2 + h + 1)
                    dve.tensor_tensor(z_t[:, cols], ps_z[:, cols], b_all[:, cols], ALU.add).then_inc(z_biased, 1)

            def uv2_low():
                dve.tensor_tensor(uv2_b[0:FF, :], ps_q[0:FF, :], uv2_a[0:FF, :].bitcast(F32),
                                  ALU.subtract).then_inc(uv_part, 1)

            def mix(m, j, over):
                t = number(m, j)
                dve.wait_ge(nb_sum, t + 1)
                if over:
                    dve.wait_ge(o_used, t * EC + EC + 1)
                dve.wait_ge(xs_ready, t + 1)
                wait(dve, yT_ps, t)
                dve.scalar_tensor_tensor(y_t, ps_a[:, :], dinv[:, bass.ds(t, 1)], xs_t, ALU.mult,
                                         ALU.add).then_inc(y_ready, 1)

            def low_part(m, j):
                t = number(m, j)
                dve.wait_ge(yT_hi, t + 1)
                dve.tensor_tensor(yt_lo[:, j % YB, :], ps_t[:, :], yt_hi[:, j % YB, :].bitcast(F32),
                                  ALU.subtract).then_inc(yT_lo, 1)

            def result(m, j):
                t = number(m, j)
                dve.wait_ge(q_ps, t + 1)
                dve.wait_ge(x1n_ready, t + 1)
                dve.tensor_tensor(x1_t[:, j, :], ps_q[:, :], x1_t[:, j, :], ALU.add).then_inc(out_ready, 1)

            def general(m, j):
                t = number(m, j)
                with dve.Fori(0, EC) as c:
                    k = t * EC + c
                    link = links(o_chain, k * 12)
                    dve.wait_ge(o_used, k + 1)
                    dve.wait_ge(o_in, k * 16 + 16)
                    dve.wait_ge(o_din, k * 16 + 16)
                    dve.bn_stats(o_st[e, 0, :], og_t[e, 0:H2])
                    link(dve.bn_stats(o_st[e, 1, :], og_t[e, H2:D]))
                    link(dve.tensor_scalar(o_late[e, :], rank1[e, bass.ds(c, 1)], float(SLOTS), None, ALU.is_gt))
                    dve.scalar_tensor_tensor(o_mine[e, :], tile_nb[e, bass.ds(c, 1)], iota_t[e, bass.ds(t, 1)],
                                             o_late[e, :], ALU.is_equal, ALU.mult)
                    link(dve.bn_aggr(o_mv[e, :], o_st[e, :, :]))
                    link(dve.tensor_scalar(o_v[e, :], o_mv[e, 1:2], EPS, None, ALU.add))
                    inverse_root(o_v[e, :], o_a[e, :], o_y[e, :], link)
                    link(dve.tensor_scalar(o_sc[e, :], o_y[e, :], 1.0 / ROOT, o_dinv[e, :], ALU.mult, ALU.mult))
                    link(dve.tensor_scalar(on_t[e, :], og_t[e, :], o_mv[e, 0:1], o_sc[e, :], ALU.subtract, ALU.mult))
                    dve.tensor_scalar(o_hot[e, :], iota_1[e, :], low1[e, bass.ds(c, 1)], o_mine[e, :],
                                      ALU.is_equal, ALU.mult).then_inc(o_ready, 1)

            def main(over):
                def step(m, j):
                    filling = isinstance(m, int) and number(m, j) == -1
                    if filling:
                        coefs(m, j)
                        neighbour_rows(0, 1)
                    tm, tj = tile(m, j, 1)
                    if exists(tm, tj):
                        if over:
                            general(tm, tj)
                        mix(tm, tj, over)
                    if filling:
                        uv2_low()
                    if exists(*tile(m, j, -1)) or exists(*tile(m, j, 2)):
                        if not filling:
                            coefs(m, j)
                    elif exists(*tile(m, j, -2)):
                        hidden_sum(*tile(m, j, -2))
                    for shift, what in ((-2, hidden_low), (2, neighbour_rows), (1, low_part), (-2, result), (0, add_bias)):
                        tm, tj = tile(m, j, shift)
                        if exists(tm, tj) and not (filling and what is neighbour_rows):
                            what(tm, tj)

                if over:
                    dve.sem_inc(o_ready, 1)
                steps(dve, step)

            dve.wait_ge(over_ready, 1)
            over = dve.value_load(over_i[0:1, 0:1], min_val=0, max_val=1)
            with dve.If(over > 0):
                main(True)
            with dve.Else():
                main(False)

        @block.tensor
        def _(pe):
            pe.wait_ge(ident_ready, 4)
            pe.wait_ge(u_in, 64)
            for r in range(RC):
                for k in range(KC):
                    mm = pe.transpose((ps_t, ps_q)[r][:, k * P:(k + 1) * P], u1_t[:, k, r * P:(r + 1) * P], ident[:, :])
            mm.then_inc(u1T_ps, 1)
            for r in range(RC):
                mm = pe.transpose(ps_z[:, r * FF:(r + 1) * FF], u2_t[0:FF, r * P:(r + 1) * P], ident[0:FF, 0:FF])
            mm.then_inc(u2T_ps, 1)
            pe.wait_ge(tiles_ready, 1)
            for g in range(EC // GROUP):
                mm = pe.matmul(ps_a[:, 0:NT * GROUP], below[0:EP, :], in_tile3[0:EP, :, g * GROUP:(g + 1) * GROUP],
                               start=(g == 0), stop=(g == EC // GROUP - 1))
            mm.then_inc(base_ready, 1)
            pe.wait_ge(u1T_sb, 2)
            for k in range(KC):
                for r in range(RC):
                    mm = pe.matmul(ps_t[:, k * FF:(k + 1) * FF], u1T[:, r, k * P:(k + 1) * P], v1_t[:, r, :],
                                   start=(r == 0), stop=(r == RC - 1))
            mm.then_inc(uv1_ps, 1)
            pe.wait_ge(u2T_sb, 2)
            for h in range(2):
                for r in range(RC):
                    mm = pe.matmul(ps_q[:, h * H2:(h + 1) * H2], u2T[:, r], v2_t[:, r, h * H2:(h + 1) * H2],
                                   start=(r == 0), stop=(r == RC - 1))
            mm.then_inc(uv2_ps, 1)
            def turns(turn):
                turn(0, False)
                for start, end in ((1, LATE), (LATE, TURNS - 1)):
                    if start < end:
                        with pe.Fori(start, end) as q:
                            turn(q, start == LATE)
                turn(TURNS - 1, True)

            def is_at(c, value):
                return isinstance(c, int) and c == value

            def degrees(g, r, late):
                pe.wait_ge(hot_ready, g + 1)
                if not late:
                    pe.wait_ge(loop_ready, g + 1)
                for k in range(GROUP):
                    c = g * GROUP + k
                    pe.matmul(ps_z[:, 0:NT], node_hot[0:EP, r, k, :], in_tile3[0:EP, :, bass.ds(c, 1)],
                              start=is_at(c, 0), stop=is_at(c, EC - 1))
                    mm = pe.matmul(ps_z[:, H2:H2 + NT], node_hot[0:EP, r, k, :],
                                   loop_hot[:, bass.ds(g, 1), k * NT:(k + 1) * NT],
                                   start=is_at(c, 0), stop=is_at(c, EC - 1))
                mm.then_inc(hot_used, 1)

            def slots(g, r):
                pe.wait_ge(slot_val_ready, g * 2 + 2)
                for k in range(GROUP):
                    c = g * GROUP + k
                    mm = pe.matmul(ps_a[:, H2:H2 + NT], slot_val[0:EP, r, k], in_tile3[0:EP, :, bass.ds(c, 1)],
                                   start=is_at(c, 0), stop=is_at(c, EC - 1))
                mm.then_inc(slot_used, 1)

            def both(q, late):
                for r in range(RING):
                    degrees(q * RING + r, r, late)
                    slots(q * RING + r, r)

            turns(both)
            pe.wait_ge(uv_part, 1)
            pe.wait_ge(most_ready, 1)
            pe.transpose(ps_t[0:1, 2 * P:3 * P], most[:, :], ident[:, :]).then_inc(most_ps, 1)
            pe.wait_ge(tq_ready, 1)
            for bank, digit in enumerate((ident[:, 0:SLOTS], ident[:, SLOTS:P])):
                for half in range(2):
                    mm = pe.matmul(ps_t[half * SLOTS:(half + 1) * SLOTS, bank * H2:bank * H2 + NT], digit, tq[:, :],
                                   start=True, stop=True)
            mm.then_inc(digits_ps, 1)
            pe.wait_ge(w_hi_ready, KC)
            pe.wait_ge(w_lo_ready, KC)
            pe.wait_ge(fold_ready, 4)

            def neighbours(m, j):
                t = number(m, j)
                pe.wait_ge(gn_lo, t + 1)
                pe.wait_ge(spread_ready, t + 1)
                wait(pe, y_ready, t)
                for h in range(2):
                    mm = pe.matmul(ps_a[:, h * H2:(h + 1) * H2], spread[:, j, :], gn_r[:, h * H2:(h + 1) * H2],
                                   start=True, stop=True)
                mm.then_inc(nb_sum, 1)

            def general(m, j):
                t = number(m, j)
                with pe.Fori(0, EC) as c:
                    pe.wait_ge(o_ready, t * EC + c + 2)
                    for h in range(2):
                        mm = pe.matmul(ps_a[:, h * H2:(h + 1) * H2], o_hot[0:EP, :], on_t[0:EP, h * H2:(h + 1) * H2],
                                       start=False, stop=True, skip_group_check=True)
                    mm.then_inc(o_used, 1)

            def product(m, j, start, stop):
                t = number(m, j)
                order = [(k, h) for k in range(KC - 2) for h in range(2)] + [(k, h) for h in range(2) for k in (KC - 2, KC - 1)]
                products = [(k, h, part) for k, h in order for part in range(3)]
                for k, h, part in products[start:stop]:
                    if k == h == part == 0:
                        pe.wait_ge(yT_lo, t + 1)
                    if k == part == 0:
                        wait(pe, z_biased, t * 2 - 1 + h)
                    y_part = (yt_hi, yt_hi, yt_lo)[part][:, j % YB, k * P:(k + 1) * P]
                    w_part = (w_hi, w_lo, w_hi)[part][:, k, h * H2:(h + 1) * H2]
                    last = k == KC - 1 and part == 2
                    mm = pe.matmul(ps_z[:, h * H2:(h + 1) * H2], y_part, w_part, start=(k == 0 and part == 0), stop=last)
                    if last:
                        mm.then_inc(z_ps, 1)

            def turn_y(m, j):
                t = number(m, j)
                pe.wait_ge(y_ready, t + 1)
                wait(pe, xT_ready, t - 2)
                for k in range(KC):
                    mm = pe.transpose(ps_t[:, k * P:(k + 1) * P], y_t[:, k * P:(k + 1) * P], ident[:, :])
                mm.then_inc(yT_ps, 1)

            def turn_x(m, j):
                t = number(m, j)
                pe.wait_ge(x1n_ready, t + 1)
                if isinstance(m, int):
                    wait(pe, yT_lo, min(t + 3, NT))
                else:
                    pe.wait_ge(yT_lo, t + 3)
                for k in range(KC):
                    mm = pe.transpose(ps_t[:, k * P:(k + 1) * P], x1n_t[:, k * P:(k + 1) * P], ident[:, :])
                mm.then_inc(xT_ps, 1)

            def ffn_in(m, j):
                t = number(m, j)
                if isinstance(m, int) and t == 0:
                    pe.wait_ge(uv_part, 3)
                pe.wait_ge(xT_lo, t + 1)
                wait(pe, out_ready, t)
                for k in range(KC):
                    mm = pe.matmul(ps_q[:, 0:2 * P], uv1[:, k], xt_r[:, k], start=(k == 0), stop=(k == KC - 1))
                mm.then_inc(h_ps, 1)

            def ffn_fold(m, j):
                t = number(m, j)
                pe.wait_ge(h_summed, t + 1)
                pe.matmul(ps_q[:, H2:H2 + P], fold[:, :], h_sum[:, :], start=True, stop=True).then_inc(h_folded, 1)

            def ffn_out(m, j):
                t = number(m, j)
                pe.wait_ge(h_ready, t * 2 + 2)
                wait(pe, out_ready, t)
                for h in range(2):
                    cols = slice(h * H2, (h + 1) * H2)
                    pe.matmul(ps_q[:, cols], h_a[:, :], uv2_a[:, cols], start=True, stop=False)
                    mm = pe.matmul(ps_q[:, cols], h_b[:, :], uv2_b[:, cols], start=False, stop=True)
                mm.then_inc(q_ps, 1)

            def main(over):
                def step(m, j):
                    now, after, before, past = (m, j), tile(m, j, 1), tile(m, j, -1), tile(m, j, -2)
                    if exists(*after):
                        neighbours(*after)
                        if over:
                            general(*after)
                    if exists(*now):
                        product(*now, 0, CUTS[0])
                    if exists(*past):
                        ffn_in(*past)
                    if exists(*after):
                        turn_y(*after)
                    if exists(*now):
                        product(*now, CUTS[0], CUTS[1])
                    if exists(*past):
                        ffn_fold(*past)
                    if exists(*now):
                        product(*now, CUTS[1], CUTS[2])
                    if exists(*past):
                        ffn_out(*past)
                    if exists(*now):
                        product(*now, CUTS[2], CUTS[3])
                    if exists(*before):
                        turn_x(*before)
                    if exists(*now):
                        product(*now, CUTS[3], 6 * KC)

                if over:
                    pe.sem_inc(o_used, 1)
                steps(pe, step)

            pe.wait_ge(over_ready, 1)
            over = pe.value_load(over_i[0:1, 0:1], min_val=0, max_val=1)
            with pe.If(over > 0):
                main(True)
            with pe.Else():
                main(False)


_INS = ["x", "src", "dst", "L0_gnn_W", "L0_gnn_b", "L0_ffn_U1", "L0_ffn_V1", "L0_ffn_b1", "L0_ffn_U2", "L0_ffn_V2",
        "L0_ffn_b2"]


def kernel(**inputs):
    import numpy as np
    import concourse.bacc as bacc
    from concourse.bass_utils import run_bass_kernel_spmd

    nc = bacc.Bacc("TRN2", target_bir_lowering=False, num_devices=1)
    arrays, args = {}, []
    for name in _INS:
        a = np.ascontiguousarray(inputs[name])
        arrays[f"in_{name}"] = a
        args.append(nc.dram_tensor(f"in_{name}", a.shape, mybir.dt.from_np(a.dtype), kind="ExternalInput").ap())
    out = nc.dram_tensor("out", inputs["x"].shape, mybir.dt.float32, kind="ExternalOutput").ap()
    gcn_ffn(nc, *args, out)
    r = run_bass_kernel_spmd(nc, [arrays], core_ids=[0])
    return r.results[0]["out"]
```
